# Optimizing a Trainium2 kernel written in Bass

```python
import numpy as np
import jax
import jax.numpy as jnp

def _softmax(x, axis=-1):
    return jax.nn.softmax(x, axis=axis)

def _gelu(x):
    return jax.nn.gelu(x, approximate=True)

def _silu(x):
    return jax.nn.silu(x)

def _sigmoid(x):
    return jax.nn.sigmoid(x)

def _layernorm(x, axis=-1, eps=1e-05):
    m = jnp.mean(x, axis=axis, keepdims=True)
    v = jnp.var(x, axis=axis, keepdims=True)
    return (x - m) / jnp.sqrt(v + eps)

def _scatter_add(tgt, idx, src, axis=0):
    return tgt.at[idx].add(src)

def _segment_sum(src, seg, n):
    return jax.ops.segment_sum(src, seg, n)
kernel_name = 'mk_adaln_d1_jaxref_r4_db5dc2'

def setup_inputs(seed: int=0):
    np.random.seed(seed)
    _w = jnp.asarray

    def _L0_attn_setup():
        import jax, jax.numpy as jnp
        import numpy as np
        NEG_INF = -1e+30
        key = jax.random.key(seed)
        k1, k2, k3 = jax.random.split(key, 3)
        B, S, D, H = (4, 512, 256, 16)
        dk = D // H
        x = jax.random.normal(k1, (B, S, D), dtype=jnp.float32)
        bound = 1.0 / np.sqrt(D)
        W_qkv = jax.random.uniform(k2, (3, H, dk, D), dtype=jnp.float32, minval=-bound, maxval=bound)
        W_o = jax.random.uniform(k3, (D, H * dk), dtype=jnp.float32, minval=-bound, maxval=bound)
        return {'x': x, 'W_qkv': W_qkv, 'W_o': W_o}
    _L0_attn_in = _L0_attn_setup()

    def _L0_ffn_setup():
        import jax, jax.numpy as jnp
        import numpy as np
        N_EMBD = 256
        EXPERT_SIZES = [(4, 256), (4, 512)]
        TOP_K = 2
        B, S = (1, 512)
        WIDTHS = []
        for count, size in EXPERT_SIZES:
            WIDTHS += [size] * count
        OFFSETS = np.concatenate([[0], np.cumsum(WIDTHS)]).astype(np.int64)
        E = len(WIDTHS)
        TOTAL_W = int(OFFSETS[-1])
        MAX_W = max(WIDTHS)

        def _stack_experts(w1, w2):
            W1e, W2e = ([], [])
            for e in range(E):
                off, wd = (int(OFFSETS[e]), WIDTHS[e])
                pad = MAX_W - wd
                W1e.append(jnp.pad(w1[:, off:off + wd], ((0, 0), (0, pad))))
                W2e.append(jnp.pad(w2[off:off + wd, :], ((0, pad), (0, 0))))
            return (jnp.stack(W1e), jnp.stack(W2e))
        key = jax.random.key(seed)
        k1, k2, k3, k4 = jax.random.split(key, 4)
        x = jax.random.normal(k1, (B, S, N_EMBD), jnp.float32)
        router_w = jax.random.normal(k2, (E, N_EMBD), jnp.float32) * 0.02
        w1 = jax.random.truncated_normal(k3, -3.0, 3.0, (N_EMBD, TOTAL_W), jnp.float32) * 0.02
        w2 = jax.random.truncated_normal(k4, -3.0, 3.0, (TOTAL_W, N_EMBD), jnp.float32) * 0.02
        return {'x': x, 'router_w': router_w, 'w1': w1, 'w2': w2}
    _L0_ffn_in = _L0_ffn_setup()
    _L0_c = _w((lambda *s: np.random.randn(*s).astype(np.float32) * 0.05)(4, 256))
    _L0_wmod = _w((lambda *s: np.random.randn(*s).astype(np.float32) * 0.05)(256, 6 * 256) * 256 ** (-0.5))
    _d = {'L0_attn_x': _L0_attn_in['x'], 'L0_attn_W_qkv': _L0_attn_in['W_qkv'], 'L0_attn_W_o': _L0_attn_in['W_o'], 'L0_ffn_router_w': _L0_ffn_in['router_w'], 'L0_ffn_w1': _L0_ffn_in['w1'], 'L0_ffn_w2': _L0_ffn_in['w2'], 'L0_c': _L0_c, 'L0_wmod': _L0_wmod}
    _x0 = _d['L0_attn_x']
    _d['L0_attn_x'] = jax.random.normal(jax.random.fold_in(jax.random.key(seed), 1), (4, 2048, 256), dtype=_x0.dtype)
    del _x0
    return _d

def reference(L0_attn_x, L0_attn_W_qkv, L0_attn_W_o, L0_ffn_router_w, L0_ffn_w1, L0_ffn_w2, L0_c, L0_wmod):

    def _L0_attn_ref(x, W_qkv, W_o):
        import jax, jax.numpy as jnp
        import numpy as np
        NEG_INF = -1e+30
        B, S, M = x.shape
        _, H, dk, _ = W_qkv.shape
        qkv = jnp.einsum('bsm,qhdm->qbhsd', x, W_qkv)
        Q, K, V = (qkv[0], qkv[1], qkv[2])
        scale = 1.0 / np.sqrt(dk)
        scores = jnp.einsum('bhqd,bhkd->bhqk', Q, K)
        causal_mask = jnp.triu(jnp.ones((S, S), dtype=bool), k=1)
        scores = jnp.where(causal_mask, NEG_INF, scores) * scale
        attn = jax.nn.softmax(scores, axis=-1)
        ctx = jnp.einsum('bhqk,bhkd->bhqd', attn, V)
        concat = jnp.transpose(ctx, (0, 2, 1, 3)).reshape(B, S, H * dk)
        return jnp.einsum('sf,df->sd'.replace('s', 'bs'), concat, W_o) if False else jnp.einsum('bsf,df->bsd', concat, W_o)

    def _L0_ffn_ref(x, router_w, w1, w2):
        import jax, jax.numpy as jnp
        import numpy as np
        N_EMBD = 256
        EXPERT_SIZES = [(4, 256), (4, 512)]
        TOP_K = 2
        B, S = (1, 512)
        WIDTHS = []
        for count, size in EXPERT_SIZES:
            WIDTHS += [size] * count
        OFFSETS = np.concatenate([[0], np.cumsum(WIDTHS)]).astype(np.int64)
        E = len(WIDTHS)
        TOTAL_W = int(OFFSETS[-1])
        MAX_W = max(WIDTHS)

        def _stack_experts(w1, w2):
            W1e, W2e = ([], [])
            for e in range(E):
                off, wd = (int(OFFSETS[e]), WIDTHS[e])
                pad = MAX_W - wd
                W1e.append(jnp.pad(w1[:, off:off + wd], ((0, 0), (0, pad))))
                W2e.append(jnp.pad(w2[off:off + wd, :], ((0, pad), (0, 0))))
            return (jnp.stack(W1e), jnp.stack(W2e))
        b, s, d = x.shape
        xf = x.reshape(-1, d)
        logits = xf @ router_w.T
        probs = jax.nn.sigmoid(logits.astype(jnp.float32))
        topw, sel = jax.lax.top_k(probs, TOP_K)
        topw = topw / (topw.sum(-1, keepdims=True) + 1e-20)
        topw = topw.astype(x.dtype)
        onehot = sel[:, :, None] == jnp.arange(E)[None, None, :]
        combine = jnp.sum(topw[:, :, None] * onehot, axis=1)
        W1e, W2e = _stack_experts(w1, w2)
        h = jnp.einsum('td,edw->tew', xf, W1e)
        h = jnp.square(jax.nn.relu(h))
        y = jnp.einsum('tew,ewd->ted', h, W2e)
        out = jnp.einsum('ted,te->td', y, combine)
        return out.reshape(b, s, d)
    x = L0_attn_x
    mod = (_silu(L0_c) @ L0_wmod).reshape(L0_c.shape[0], 6, 1, -1)
    sa, ca, ga, sb, cb, gb = (mod[:, 0], mod[:, 1], mod[:, 2], mod[:, 3], mod[:, 4], mod[:, 5])
    ga = (2 * (ga >= 0) - 1) * jnp.maximum(jnp.abs(ga), 0.25)
    gb = (2 * (gb >= 0) - 1) * jnp.maximum(jnp.abs(gb), 0.25)
    h = _layernorm(x, axis=-1) * (1 + ca) + sa
    x = x + ga * _L0_attn_ref(h, L0_attn_W_qkv, L0_attn_W_o)
    h = _layernorm(x, axis=-1) * (1 + cb) + sb
    x = x + gb * _L0_ffn_ref(h, L0_ffn_router_w, L0_ffn_w1, L0_ffn_w2)
    return x

_drawn_inputs = setup_inputs


def setup_inputs(seed=0):
    import zlib

    import numpy as np

    out = dict(_drawn_inputs(seed))
    spreads = {}
    factors = {'L0_attn_W_qkv': 8.0,
     'L0_attn_W_o': 8.0,
     'L0_ffn_router_w': 7.796,
     'L0_ffn_w1': 7.461,
     'L0_ffn_w2': 6.823,
     'L0_c': 5.581,
     'L0_wmod': 5.455}
    for name, (base, spread) in spreads.items():
        noise = np.random.default_rng([zlib.crc32(name.encode()), seed]).standard_normal(out[name].shape)
        drawn = base * np.exp(spread * noise) if base else spread * noise
        out[name] = jnp.asarray(drawn.astype(out[name].dtype))
    for name, factor in factors.items():
        out[name] = (out[name] * factor).astype(out[name].dtype)
    return out
```

```python
from contextlib import ExitStack

import concourse.bass as bass
from concourse import mybir

F32 = mybir.dt.float32
BF16 = mybir.dt.bfloat16
ALU = mybir.AluOpType
ACT = mybir.ActivationFunctionType
AX = mybir.AxisListType

P = 128
B, S, D, H = 4, 2048, 256, 16
DK = D // H
T = B * S
KK = D // P
TB = 512
TT = TB // P
NBLK = T // TB
BPB = S // TB
SCALE = DK ** -0.5
EPS = 1e-5
NEG = -1e30

HG = 4
NG = B * H // HG
QT = S // P
PARTS = 3
STACK = 6 * DK
VW = 2 * DK

WIDTHS = [256] * 4 + [512] * 4
E = len(WIDTHS)
FT = [w // P for w in WIDTHS]
NW = sum(FT)
EXPERT = [e for e in range(E) for _ in range(FT[e])]
FIRST_W = [sum(FT[:e]) for e in range(E)]

UNITS = [(j, kt, max(0, kt - TT * j) * P) for j in range(BPB) for kt in range(TT * (j + 1))]
NU = len(UNITS)
NS = HG * NU
DIAG = [kt >= TT * j for j, kt, _ in UNITS]
UNITS_TO = [TT * (j + 1) * (j + 2) // 2 for j in range(BPB)]
FIRST = 1
LAG = 2
SB = 3
PB = 4

CW = 1024
CHUNKS = [
    (h, t, k0, min(CW, P * (t + 1) - k0), k0 + CW >= P * (t + 1))
    for h in range(HG) for t in range(QT) for k0 in range(0, P * (t + 1), CW)
]
NC = len(CHUNKS)


def chunk_plan():
    first, last = PLAN_FIRST, PLAN_LAST
    cost = [(TB - UNITS[n // 3][2] + 128) / 3 for n in range(3 * NU)]
    span = sum(cost[3 * first:3 * last])
    total = sum(w + 128 for *_, w, _ in CHUNKS)
    plan, c, done, spent = [[] for _ in cost], 0, 0, 0
    for n in range(3 * first, 3 * last):
        spent += cost[n]
        while c < NC and done * span < spent * total:
            plan[n].append(c)
            done += CHUNKS[c][3] + 128
            c += 1
    plan[3 * last - 1] += range(c, NC)
    return plan


PLAN_FIRST, PLAN_LAST = 1, NU - 4
PLAN = chunk_plan()


def count_from_first(nc, counts):
    with nc.Block() as block:
        @block.sync
        def _(sp):
            for s in counts[0::4]:
                sp.sem_inc(s, FIRST)

        @block.scalar
        def _(act):
            for s in counts[1::4]:
                act.sem_inc(s, FIRST)

        @block.vector
        def _(dve):
            for s in counts[2::4]:
                dve.sem_inc(s, FIRST)

        @block.gpsimd
        def _(pool):
            for s in counts[3::4]:
                pool.sem_inc(s, FIRST)

    counts.clear()


def wait_apart(engine, semaphore, value, passed):
    engine.wait_ge(semaphore, value)
    engine.sem_inc(passed, 1)


def following(p, i):
    return 1 - p, i + p


def adaln_layer(nc, x, wqkv_t, wo_t, rw_t, w1, w2, c_t, wmod, out):
    q_parts = nc.dram_tensor("q_parts", (D, PARTS, T), BF16, kind="Internal").ap()
    k_parts = nc.dram_tensor("k_parts", (D, PARTS, T), BF16, kind="Internal").ap()
    v_ones = nc.dram_tensor("v_ones", (T, H * VW), F32, kind="Internal").ap()
    contexts = nc.dram_tensor("contexts", (H * VW, T), F32, kind="Internal").ap()

    with ExitStack() as whole:
        def sb(name, shape, dt=F32, at=whole):
            return at.enter_context(nc.sbuf_tensor(name, shape, dt))

        def sem(name):
            return whole.enter_context(nc.semaphore(name))

        counts = []

        def sems(name, n=2):
            made = [sem(f"{name}{k}") for k in range(n)]
            counts.extend(made)
            return made

        ps = whole.enter_context(nc.psum_tensor("ps", [P, 8 * 512], F32))

        def bank(n, count=1):
            return ps[:, n * 512:(n + count) * 512]

        w1_s = sb("w1_s", [P, KK, NW * P])
        w2_s = sb("w2_s", [P, NW, D])
        wo_s = sb("wo_s", [P, KK, D])
        rw_s = sb("rw_s", [P, KK, E])
        ident = sb("ident", [P, P])
        mod_t = sb("mod_t", [P, 4, KK, B])
        gates = sb("gates", [P, B, 2 * D])

        w_in = sem("w_in")
        block1(nc, sb, sem, sems, counts, bank, x, wqkv_t, wo_t, rw_t, w1, w2, c_t, wmod, q_parts, k_parts, v_ones,
               w1_s, w2_s, wo_s, rw_s, ident, mod_t, gates, w_in)
        block2(nc, sb, sem, sems, counts, bank, q_parts, k_parts, v_ones, contexts, ident)
        block3(nc, sb, sem, sems, counts, bank, x, contexts, w1_s, w2_s, wo_s, rw_s, ident, mod_t, gates, w_in, out)


def preceding(p, i):
    return 1 - p, i + p - 1


def block1(nc, sb_, sem, sems, counts, bank, x, wqkv_t, wo_t, rw_t, w1, w2, c_t, wmod, q_parts, k_parts, v_ones,
           w1_s, w2_s, wo_s, rw_s, ident, mod_t, gates, w_in):
    with ExitStack() as own:
        def sb(name, shape, dt=F32):
            return sb_(name, shape, dt, own)

        wqkv_s = sb("wqkv_s", [P, KK, 3 * D])
        wmod_s = sb("wmod_s", [P, KK, 6 * D])
        ct = sb("ct", [P, KK, B])
        ce = sb("ce", [P, KK, B])
        silu = sb("silu", [P, KK, B])
        silu_all = sb("silu_all", [P, KK, B, P])
        sign = sb("sign", [P, B, 2 * D])
        size = sb("size", [P, B, 2 * D])
        xin = [sb(f"xin{p}", [P, TT, D]) for p in range(2)]
        stats = [sb(f"stats{p}", [P, TT, 6]) for p in range(2)]
        mv = [sb(f"mv{p}", [P, TT, 2]) for p in range(2)]
        rstd = [sb(f"rstd{p}", [P, TT]) for p in range(2)]
        xn = [sb(f"xn{p}", [P, TT, D]) for p in range(2)]
        ht = [sb(f"ht{p}", [P, KK, TB]) for p in range(2)]
        rest = sb("rest", [P, 4, TB])
        parts = [sb(f"parts{p}", [P, 4, PARTS, TB], BF16) for p in range(2)]
        vt = [sb(f"vt{p}", [P, TT, H, VW]) for p in range(2)]

        setup_in = sem("setup_in")
        id_zero, id_done = sem("id_zero"), sem("id_done")
        c_steps, c_exp = sem("c_steps"), sem("c_exp")
        mod_mm, gate_mm = sem("mod_mm"), sem("gate_mm")
        gate_steps = sem("gate_steps")
        ones_set = sem("ones_set")
        x_in, stat_done, xn_done = sems("x_in"), sems("stat_done"), sems("xn_done")
        rooted, inverted = sems("rooted"), sems("inverted")
        t_mm, ht_done = sems("t_mm"), sems("ht_done")
        qk_mm, part1, rest1, part2, part3 = (sems(n) for n in ("qk_mm", "part1_", "rest1_", "part2_", "part3_"))
        v_mm, v_done = sems("v_mm"), sems("v_done")
        stored = sems("stored")

        sp_passed, dve_passed = sem("sp_passed"), sem("dve_passed")
        count_from_first(nc, counts)
        with nc.Block() as block:
            @block.sync
            def _(sp):
                sp.dma_start(ct[:, :, :], c_t.rearrange("(k p) b -> p k b", p=P)).then_inc(setup_in, 16)
                sp.dma_start(wmod_s[:, :, :], wmod.rearrange("(k p) n -> p k n", p=P)).then_inc(setup_in, 16)
                sp.dma_start(wqkv_s[:, :, :], wqkv_t.rearrange("(k p) n -> p k n", p=P)).then_inc(setup_in, 16)

                def store(p, i):
                    cols = bass.ds((2 * i + p) * TB, TB)
                    for o in range(4):
                        to = (q_parts, k_parts)[o // 2]
                        wait_apart(sp, part3[p], FIRST + 4 * i + o + 1, sp_passed)
                        sp.dma_start(to[P * (o % 2):P * (o % 2 + 1), :, cols],
                                     parts[p][:, o, :, :]).then_inc(stored[p], 16)
                    wait_apart(sp, v_done[p], FIRST + 2 * (i + 1), sp_passed)
                    sp.dma_start(v_ones[cols, :].rearrange("(t p) c -> p t c", p=P),
                                 vt[p][:, :, :, :].rearrange("p t h c -> p t (h c)")).then_inc(stored[p], 16)

                sp.dma_start(wo_s[:, :, :], wo_t.rearrange("(k p) n -> p k n", p=P)).then_inc(w_in, 16)
                sp.dma_start(rw_s[:, :, :], rw_t.rearrange("(k p) n -> p k n", p=P)).then_inc(w_in, 16)
                sp.dma_start(w1_s[:, :, :], w1.rearrange("(k p) n -> p k n", p=P)).then_inc(w_in, 16)
                sp.dma_start(w2_s[:, :, :], w2.rearrange("(k p) n -> p k n", p=P)).then_inc(w_in, 16)
                with sp.Fori(0, NBLK // 2) as i:
                    for p in range(2):
                        store(p, i)
                for p in range(2):
                    sp.wait_ge(stored[p], FIRST + 16 * 5 * NBLK // 2)

            @block.gpsimd
            def _(pool):
                nc.gpsimd.memset(ident[:, :], 0.0).then_inc(id_zero, 1)
                pool.wait_ge(id_zero, 1)
                nc.gpsimd.affine_select(out=ident[:, :], in_=ident[:, :], compare_op=ALU.not_equal, fill=1.0,
                                        base=0, pattern=[[-1, P]], channel_multiplier=1).then_inc(id_done, 1)
                for p in range(2):
                    nc.gpsimd.memset(vt[p][:, :, :, DK:VW], 1.0).then_inc(ones_set, 1)

            @block.scalar
            def _(act):
                def load(p, i):
                    act.wait_ge(xn_done[p], FIRST + TT * i)
                    src = x[bass.ds((2 * i + p) * TB, TB), :].rearrange("(t p) d -> p t d", p=P)
                    act.dma_start(xin[p][:, :, :], src).then_inc(x_in[p], 16)

                load(0, 0)
                load(1, 0)
                act.wait_ge(setup_in, 48)
                nc.scalar.activation(ce[:, :, :], ct[:, :, :], ACT.Exp, scale=-1.0).then_inc(c_exp, 1)
                act.wait_ge(ones_set, 2)

                def part_1(p, i, o):
                    act.wait_ge(qk_mm[p], FIRST + 4 * i + o + 1)
                    if o == 0:
                        act.wait_ge(stored[p], FIRST + 80 * i)
                    nc.scalar.activation(parts[p][:, o, 0, :], bank(2 + o), ACT.Copy).then_inc(part1[p], 1)

                def part_2(p, i, o):
                    act.wait_ge(rest1[p], FIRST + 4 * i + o + 1)
                    nc.scalar.activation(parts[p][:, o, 1, :], rest[:, o, :], ACT.Copy).then_inc(part2[p], 1)

                def values(p, i, half):
                    act.wait_ge(v_mm[p], FIRST + 2 * i + half + 1)
                    nc.scalar.activation(
                        vt[p][:, 2 * half:2 * half + 2, :, 0:DK],
                        bank(6 + half).rearrange("p (t h c) -> p t h c", t=2, h=H), ACT.Copy).then_inc(v_done[p], 1)

                def root(p, i):
                    act.wait_ge(stat_done[p], FIRST + 9 * (i + 1))
                    nc.scalar.activation(rstd[p][:, :], rstd[p][:, :], ACT.Sqrt).then_inc(rooted[p], 1)

                def step(p, i, more=True, loads=True):
                    if loads:
                        load(p, i + 1)
                    part_1(p, i, 0)
                    for o in range(1, 4):
                        part_1(p, i, o)
                        part_2(p, i, o - 1)
                        if o == 1 and more:
                            root(*following(p, i))
                    part_2(p, i, 3)
                    for half in range(2):
                        values(p, i, half)

                root(0, 0)
                last = NBLK // 2 - 1
                with act.Fori(0, last) as i:
                    for p in range(2):
                        step(p, i)
                step(0, last, loads=False)
                step(1, last, more=False, loads=False)

            @block.vector
            def _(dve):
                dve.wait_ge(c_exp, 1)
                nc.vector.tensor_scalar(ce[:, :, :], ce[:, :, :], 1.0, None, ALU.add).then_inc(c_steps, 1)
                dve.wait_ge(c_steps, 1)
                nc.vector.reciprocal(ce[:, :, :], ce[:, :, :]).then_inc(c_steps, 1)
                dve.wait_ge(c_steps, 2)
                nc.vector.tensor_tensor(silu[:, :, :], ct[:, :, :], ce[:, :, :], ALU.mult).then_inc(c_steps, 1)
                dve.wait_ge(c_steps, 3)
                nc.vector.tensor_copy(silu_all[:, :, :, :], silu[:, :, :].unsqueeze(3).to_broadcast([P, KK, B, P])
                                      ).then_inc(c_steps, 1)

                def gate_guard():
                    dve.wait_ge(gate_mm, 1)
                    g = bank(0, B).rearrange("p (b n) -> p b n", b=B)
                    nc.vector.tensor_scalar(sign[:, :, :], g, 0.0, 2.0, ALU.is_ge, ALU.mult).then_inc(gate_steps, 1)
                    dve.wait_ge(gate_steps, 1)
                    nc.vector.scalar_tensor_tensor(out=size[:, :, :], in0=sign[:, :, :], scalar=1.0, in1=g,
                                                   op0=ALU.subtract, op1=ALU.mult).then_inc(gate_steps, 1)
                    dve.wait_ge(gate_steps, 2)
                    nc.vector.tensor_scalar(size[:, :, :], size[:, :, :], 0.25, None, ALU.max
                                            ).then_inc(gate_steps, 1)
                    dve.wait_ge(gate_steps, 3)
                    nc.vector.scalar_tensor_tensor(out=gates[:, :, :], in0=sign[:, :, :], scalar=1.0,
                                                   in1=size[:, :, :], op0=ALU.subtract, op1=ALU.mult
                                                   ).then_inc(gate_steps, 1)
                    dve.wait_ge(mod_mm, 1)
                    m = bank(4)[:, 0:4 * KK * B].rearrange("p (w k b) -> p w k b", w=4, k=KK)
                    for w in range(4):
                        nc.vector.tensor_scalar(mod_t[:, w], m[:, w], float(w % 2), None, ALU.add
                                                ).then_inc(gate_steps, 1)
                    dve.wait_ge(gate_steps, 8)

                def variance(p, i):
                    dve.wait_ge(x_in[p], FIRST + 16 * (i + 1))
                    for t in range(TT):
                        nc.vector.bn_stats(stats[p][:, t, :], xin[p][:, t, :]).then_inc(stat_done[p], 1)
                    for t in range(TT):
                        wait_apart(dve, stat_done[p], FIRST + 9 * i + t + 1, dve_passed)
                        nc.vector.bn_aggr(mv[p][:, t, :], stats[p][:, t, :]).then_inc(stat_done[p], 1)
                    dve.wait_ge(stat_done[p], FIRST + 9 * i + 8)
                    nc.vector.tensor_scalar(rstd[p][:, :], mv[p][:, :, 1], EPS, None, ALU.add
                                            ).then_inc(stat_done[p], 1)

                def normalise(p, i):
                    dve.wait_ge(rooted[p], FIRST + i + 1)
                    nc.vector.reciprocal(rstd[p][:, :], rstd[p][:, :]).then_inc(inverted[p], 1)
                    dve.wait_ge(inverted[p], FIRST + i + 1)
                    dve.wait_ge(t_mm[p], FIRST + 2 * i)
                    for t in range(TT):
                        nc.vector.tensor_scalar(xn[p][:, t, :], xin[p][:, t, :], mv[p][:, t, 0:1],
                                                rstd[p][:, t:t + 1], ALU.subtract, ALU.mult).then_inc(xn_done[p], 1)

                def modulate(p, i, b):
                    dve.wait_ge(v_mm[p], FIRST + 2 * i)
                    for k in range(KK):
                        dve.wait_ge(t_mm[p], FIRST + 2 * i + k + 1)
                        nc.vector.tensor_scalar(ht[p][:, k, :], bank(k), mod_t[:, 1, k, bass.ds(b, 1)],
                                                mod_t[:, 0, k, bass.ds(b, 1)], ALU.mult, ALU.add
                                                ).then_inc(ht_done[p], 1)

                def rest_1(p, i, o):
                    dve.wait_ge(part1[p], FIRST + 4 * i + o + 1)
                    dve.wait_ge(part3[1 - p], FIRST + 4 * (i + p))
                    nc.vector.tensor_tensor(rest[:, o, :], bank(2 + o), parts[p][:, o, 0, :], ALU.subtract
                                            ).then_inc(rest1[p], 1)

                def part_3(p, i, o):
                    dve.wait_ge(part2[p], FIRST + 4 * i + o + 1)
                    nc.vector.tensor_tensor(parts[p][:, o, 2, :], rest[:, o, :], parts[p][:, o, 1, :], ALU.subtract
                                            ).then_inc(part3[p], 1)

                def step(p, i, b, more=True):
                    rest_1(p, i, 0)
                    if more:
                        variance(*following(p, i))
                    rest_1(p, i, 1)
                    part_3(p, i, 0)
                    if more:
                        normalise(*following(p, i))
                    rest_1(p, i, 2)
                    part_3(p, i, 1)
                    rest_1(p, i, 3)
                    if more:
                        modulate(*following(p, i), b)
                    part_3(p, i, 2)
                    part_3(p, i, 3)

                variance(0, 0)
                gate_guard()
                normalise(0, 0)
                modulate(0, 0, 0)
                last = NBLK // 2 - 1
                with dve.Fori(0, last) as i:
                    for p in range(2):
                        step(p, i, (i + p) // (BPB // 2))
                step(0, last, B - 1)
                step(1, last, B - 1, more=False)

            @block.tensor
            def _(pe):
                pe.wait_ge(setup_in, 48)
                pe.wait_ge(id_done, 1)
                pe.wait_ge(c_steps, 4)
                for b in range(B):
                    for g, off in ((0, 2 * D), (1, 5 * D)):
                        for k in range(KK):
                            mm = nc.tensor.matmul(bank(b)[:, g * D:(g + 1) * D], silu_all[:, k, b, :],
                                                  wmod_s[:, k, off:off + D], start=(k == 0), stop=(k == KK - 1))
                mm.then_inc(gate_mm, 1)
                for w, which in enumerate((0, 1, 3, 4)):
                    for half in range(KK):
                        for k in range(KK):
                            c0 = which * D + half * P
                            n0 = (w * KK + half) * B
                            mm = nc.tensor.matmul(bank(4)[:, n0:n0 + B], wmod_s[:, k, c0:c0 + P],
                                                  silu[:, k, :], start=(k == 0), stop=(k == KK - 1))
                mm.then_inc(mod_mm, 1)
                pe.wait_ge(gate_steps, 8)

                def transposes(p, i):
                    pe.wait_ge(ht_done[1 - p], FIRST + 2 * (i + p))
                    pe.wait_ge(xn_done[p], FIRST + TT * (i + 1))
                    for k in range(KK):
                        for t in range(TT):
                            mm = nc.tensor.transpose(bank(k)[:, t * P:(t + 1) * P],
                                                     xn[p][:, t, k * P:(k + 1) * P], ident[:, :])
                        mm.then_inc(t_mm[p], 1)

                def queries_keys(p, i):
                    pe.wait_ge(ht_done[p], FIRST + KK * (i + 1))
                    for o in range(4):
                        pe.wait_ge(rest1[1 - p], FIRST + 4 * (i + p))
                        for k in range(KK):
                            mm = nc.tensor.matmul(bank(2 + o), wqkv_s[:, k, o * P:(o + 1) * P], ht[p][:, k, :],
                                                  start=(k == 0), stop=(k == KK - 1))
                        mm.then_inc(qk_mm[p], 1)

                def values(p, i):
                    pe.wait_ge(v_done[1 - p], FIRST + 2 * (i + p))
                    for t in range(TT):
                        o = bank(6 + t // 2)[:, (t % 2) * D:(t % 2 + 1) * D]
                        for k in range(KK):
                            mm = nc.tensor.matmul(o, ht[p][:, k, t * P:(t + 1) * P], wqkv_s[:, k, 2 * D:3 * D],
                                                  start=(k == 0), stop=(k == KK - 1))
                        if t % 2:
                            mm.then_inc(v_mm[p], 1)

                def step(p, i, more=True):
                    queries_keys(p, i)
                    if more:
                        transposes(*following(p, i))
                    values(p, i)

                transposes(0, 0)
                last = NBLK // 2 - 1
                with pe.Fori(0, last) as i:
                    for p in range(2):
                        step(p, i)
                step(0, last)
                step(1, last, more=False)


def block2(nc, sb_, sem, sems, counts, bank, q_parts, k_parts, v_ones, contexts, ident):
    with ExitStack() as own:
        def sb(name, shape, dt=F32):
            return sb_(name, shape, dt, own)

        qs = [sb(f"qs{p}", [STACK + PARTS, HG, S], BF16) for p in range(2)]
        ks = [sb(f"ks{p}", [STACK + PARTS, HG, S], BF16) for p in range(2)]
        vs = [sb(f"vs{p}", [P, QT, HG, VW]) for p in range(2)]
        probs = [sb(f"probs{k}", [P, HG, TB]) for k in range(PB)]
        causal = sb("causal", [P, CW])
        causal_b = sb("causal_b", [P, P], BF16)
        ident_b = sb("ident_b", [P, P], BF16)
        junk = [sb(f"junk{k}", [P, CW], BF16) for k in range(2)]
        maxima = [sb(f"maxima{p}", [P, HG, QT]) for p in range(2)]
        early = sb("early", [P, HG, QT // 2])
        neg = [sb(f"neg{p}", [HG * QT, PARTS, P], BF16) for p in range(2)]
        neg_rest = sb("neg_rest", [HG * QT, P])
        ctx_out = [sb(f"ctx_out{k}", [P, TB]) for k in range(2)]

        causal_set = sem("causal_set")
        mask_set = sem("mask_set")
        ones_set = sem("k_ones_set")
        heads_in = [sems(f"heads_in{p}_", HG) for p in range(2)]
        v_in = sems("v_in")
        max_mm, max_done = sems("max_mm"), sems("max_done")
        max_all, max_t = sems("max_all"), sems("max_t")
        neg_done, neg_in = sems("neg_done"), sems("neg_in")
        s_mm, exp_done = sems("s_mm"), sems("exp_done")
        pv_mm, ctx_done = sems("pv_mm"), sems("ctx_done")
        ctx_stored = sems("ctx_stored")
        last = NG // 2 - 1

        def place(p, i):
            per = B * H // HG // B
            return (2 * i + p) // per if isinstance(i, int) else i // (per // 2), (i % (per // 2)) * 2 + p

        sp_passed, dve_passed, pe_passed = (sem(f"{n}_passed_a") for n in ("sp", "dve", "pe"))
        count_from_first(nc, counts)
        with nc.Block() as block:
            @block.sync
            def _(sp):
                def load(p, i):
                    b, hg = place(p, i)
                    wait_apart(sp, s_mm[p], FIRST + NS * i, sp_passed)
                    for h in range(HG):
                        rows = bass.ds((hg * HG + h) * DK, DK)
                        toks = bass.ds(b * S, S)
                        for side, src, same in ((qs[p], q_parts, False), (ks[p], k_parts, True)):
                            for r0, n, other in ((0, 3, 0), (3 * DK, 2, 1), (5 * DK, 1, 2)):
                                if same:
                                    s = src[rows, other:other + 1, toks].to_broadcast([DK, n, S])
                                else:
                                    s = src[rows, 0:n, toks]
                                sp.dma_start(side[r0:r0 + n * DK, h, :], s).then_inc(heads_in[p][h], 16)

                def load_v(p, i):
                    b, hg = place(p, i)
                    wait_apart(sp, pv_mm[p], FIRST + NU * i, sp_passed)
                    src = v_ones[bass.ds(b * S, S), bass.ds(hg * (HG * VW), HG * VW)]
                    sp.dma_start(vs[p][:, :, :, :].rearrange("p t h c -> p t (h c)"),
                                 src.rearrange("(t p) c -> p t c", p=P)).then_inc(v_in[p], 16)

                def store(p, i, j):
                    b, hg = place(p, i)
                    wait_apart(sp, ctx_done[p], FIRST + BPB * i + j + 1, sp_passed)
                    sp.dma_start(contexts[bass.ds(hg * P, P), bass.ds(b * S + j * TB, TB)],
                                 ctx_out[j % 2][:, :]).then_inc(ctx_stored[j % 2], 16)

                def put_neg(p, i):
                    wait_apart(sp, neg_done[p], FIRST + 4 * (i + 1), sp_passed)
                    for n in range(PARTS):
                        sp.dma_start(qs[p][STACK + n:STACK + n + 1, :, :].rearrange("a h (t c) -> a (h t) c", c=P),
                                     neg[p][:, n, :]).then_inc(neg_in[p], 16)

                def step(p, i, before=True, more=True):
                    if more:
                        load(*following(p, i))
                    if before:
                        store(*preceding(p, i), BPB - 1)
                    if more:
                        load_v(*following(p, i))
                    for j in range(BPB - 1):
                        store(p, i, j)
                    if more:
                        put_neg(*following(p, i))

                load(0, 0)
                load_v(0, 0)
                put_neg(0, 0)
                step(0, 0, before=False)
                with sp.Fori(0, last) as i:
                    step(1, i)
                    step(0, i + 1)
                step(1, last, more=False)
                store(1, last, BPB - 1)
                for k in range(2):
                    sp.wait_ge(ctx_stored[k], FIRST + 16 * NG * BPB // 2)

            @block.gpsimd
            def _(pool):
                nc.gpsimd.memset(causal[:, :], 0.0).then_inc(causal_set, 1)
                pool.wait_ge(causal_set, 1)
                nc.gpsimd.affine_select(out=causal[:, CW - P:CW], in_=causal[:, CW - P:CW], compare_op=ALU.is_ge,
                                        fill=NEG, base=0, pattern=[[-1, P]], channel_multiplier=1
                                        ).then_inc(causal_set, 1)
                pool.wait_ge(causal_set, 2)
                for p in range(2):
                    pool.wait_ge(ones_set, p)
                    nc.gpsimd.memset(ks[p][STACK:STACK + PARTS, :, :], 1.0).then_inc(ones_set, 1)

            @block.scalar
            def _(act):
                def context(p, i, j):
                    act.wait_ge(pv_mm[p], FIRST + NU * i + UNITS_TO[j])
                    act.wait_ge(ctx_stored[j % 2], FIRST + 16 * (4 * i + 2 * p + j // 2))
                    nc.scalar.activation(ctx_out[j % 2][:, :], bank(3), ACT.Copy).then_inc(ctx_done[p], 1)

                def step(p, i, before=True):
                    for u, (j, kt, q0) in enumerate(UNITS):
                        if u >= PB:
                            act.wait_ge(pv_mm[p], FIRST + NU * i + u - PB + 1)
                        elif before:
                            act.wait_ge(pv_mm[1 - p], FIRST + NU * (i + p) + u - PB + 1)
                        for h in range(HG):
                            if h == 2 and u == LAG - 1 and before:
                                context(*preceding(p, i), BPB - 1)
                            if h == 2 and u - LAG + 1 in UNITS_TO:
                                context(p, i, UNITS_TO.index(u - LAG + 1))
                            n = HG * u + h
                            act.wait_ge(s_mm[p], FIRST + NS * i + n + 1)
                            nc.scalar.activation(probs[u % PB][:, h, q0:TB], bank(n % SB)[:, q0:TB], ACT.Exp,
                                                 scale=SCALE).then_inc(exp_done[p], 1)

                step(0, 0, before=False)
                with act.Fori(0, last) as i:
                    step(1, i)
                    step(0, i + 1)
                step(1, last)
                context(1, last, BPB - 1)

            @block.vector
            def _(dve):
                dve.wait_ge(causal_set, 2)
                nc.vector.tensor_copy(causal_b[:, :], causal[:, CW - P:CW]).then_inc(mask_set, 1)
                nc.vector.tensor_copy(ident_b[:, :], ident[:, :]).then_inc(mask_set, 1)

                def maxima_of(p, i):
                    for c, (h, t, k0, w, end) in enumerate(CHUNKS):
                        if c >= 2:
                            dve.wait_ge(max_done[p], FIRST + NC * i + c - 1)
                        wait_apart(dve, max_mm[p], FIRST + NC * i + c + 1, dve_passed)
                        tile = bank(4 + 2 * (c % 2), 2)[:, 0:w]
                        if end:
                            nc.vector.tensor_tensor_reduce(
                                junk[c % 2][:, 0:w], tile, causal[:, CW - w:CW], 1.0, -3e38, ALU.add, ALU.max,
                                maxima[p][:, h, t:t + 1]).then_inc(max_done[p], 1)
                        else:
                            nc.vector.tensor_reduce(early[:, h, t - QT // 2:t - QT // 2 + 1], tile, AX.X, ALU.max
                                                    ).then_inc(max_done[p], 1)
                    dve.wait_ge(max_done[p], FIRST + NC * (i + 1))
                    late = maxima[p][:, :, QT // 2:QT]
                    nc.vector.tensor_tensor(late, late, early[:, :, :], ALU.max).then_inc(max_all[p], 1)
                    dve.wait_ge(max_t[p], FIRST + i + 1)
                    dve.wait_ge(neg_in[p], FIRST + 48 * i)
                    m = bank(4)[0:HG * QT, 0:P]
                    nc.vector.tensor_scalar(neg[p][:, 0, :], m, -1.0, None, ALU.mult).then_inc(neg_done[p], 1)
                    dve.wait_ge(neg_done[p], FIRST + 4 * i + 1)
                    nc.vector.scalar_tensor_tensor(out=neg_rest[:, :], in0=m, scalar=-1.0, in1=neg[p][:, 0, :],
                                                   op0=ALU.mult, op1=ALU.subtract).then_inc(neg_done[p], 1)
                    dve.wait_ge(neg_done[p], FIRST + 4 * i + 2)
                    nc.vector.tensor_copy(neg[p][:, 1, :], neg_rest[:, :]).then_inc(neg_done[p], 1)
                    dve.wait_ge(neg_done[p], FIRST + 4 * i + 3)
                    nc.vector.tensor_tensor(neg[p][:, 2, :], neg_rest[:, :], neg[p][:, 1, :], ALU.subtract
                                            ).then_inc(neg_done[p], 1)

                maxima_of(0, 0)
                with dve.Fori(0, last) as i:
                    for p in range(2):
                        maxima_of(*following(p, i))
                maxima_of(1, last)

            @block.tensor
            def _(pe):
                pe.wait_ge(ones_set, 2)
                pe.wait_ge(mask_set, 2)

                def max_chunk(p, i, c):
                    h, t, k0, w, _ = CHUNKS[c]
                    if t == 0:
                        pe.wait_ge(heads_in[p][h], FIRST + 96 * (i + 1))
                    if c >= 2:
                        pe.wait_ge(max_done[p], FIRST + NC * i + c - 1)
                    elif c == 0:
                        pe.wait_ge(neg_done[1 - p], FIRST + 4 * (i + p))
                    for m0 in range(0, w, 512):
                        n = min(512, w - m0)
                        mm = nc.tensor.matmul(bank(4 + 2 * (c % 2), 2)[:, m0:m0 + n],
                                              qs[p][0:STACK, h, t * P:(t + 1) * P],
                                              ks[p][0:STACK, h, k0 + m0:k0 + m0 + n], start=True, stop=True)
                    mm.then_inc(max_mm[p], 1)

                def max_turn(p, i):
                    wait_apart(pe, max_all[p], FIRST + i + 1, pe_passed)
                    nc.tensor.transpose(bank(4)[0:HG * QT, 0:P], maxima[p][:, :, :].rearrange("p h t -> p (h t)"),
                                        ident[:, :]).then_inc(max_t[p], 1)

                def score(p, i, u, h):
                    j, kt, q0 = UNITS[u]
                    n = HG * u + h
                    if n == 0:
                        pe.wait_ge(neg_in[p], FIRST + 48 * (i + 1))
                        pe.wait_ge(exp_done[1 - p], FIRST + NS * (i + p))
                    elif n >= SB:
                        pe.wait_ge(exp_done[p], FIRST + NS * i + n - SB + 1)
                    mm = nc.tensor.matmul(bank(n % SB)[:, q0:TB], ks[p][:, h, kt * P:(kt + 1) * P],
                                          qs[p][:, h, j * TB + q0:(j + 1) * TB], start=True, stop=not DIAG[u])
                    if DIAG[u]:
                        mm = nc.tensor.matmul(bank(n % SB)[:, q0:q0 + P], causal_b[:, :], ident_b[:, :],
                                              start=False, stop=True)
                    mm.then_inc(s_mm[p], 1)

                def p_v(p, i, u):
                    j, kt, q0 = UNITS[u]
                    if u == 0:
                        pe.wait_ge(v_in[p], FIRST + 16 * (i + 1))
                        pe.wait_ge(ctx_done[1 - p], FIRST + BPB * (i + p))
                    elif kt == 0:
                        pe.wait_ge(ctx_done[p], FIRST + BPB * i + j)
                    pe.wait_ge(exp_done[p], FIRST + NS * i + HG * (u + 1))
                    for h in range(HG):
                        mm = nc.tensor.matmul(bank(3)[VW * h:VW * (h + 1), q0:TB], vs[p][:, kt, h, :],
                                              probs[u % PB][:, h, q0:TB], start=(kt == 0),
                                              stop=(kt == TT * (j + 1) - 1))
                    mm.then_inc(pv_mm[p], 1)

                def step(p, i, before=True, more=True):
                    def chunks(n):
                        if more:
                            for c in PLAN[n]:
                                max_chunk(*following(p, i), c)

                    for u in range(NU):
                        score(p, i, u, 0)
                        score(p, i, u, 1)
                        chunks(3 * u)
                        if u >= LAG:
                            p_v(p, i, u - LAG)
                        elif before:
                            p_v(*preceding(p, i), NU - LAG + u)
                        chunks(3 * u + 1)
                        score(p, i, u, 2)
                        score(p, i, u, 3)
                        chunks(3 * u + 2)
                        if more and u == PLAN_LAST + 1:
                            max_turn(*following(p, i))

                for c in range(NC):
                    max_chunk(0, 0, c)
                max_turn(0, 0)
                step(0, 0, before=False)
                with pe.Fori(0, last) as i:
                    step(1, i)
                    step(0, i + 1)
                step(1, last, more=False)
                for u in range(NU - LAG, NU):
                    p_v(1, last, u)


def block3(nc, sb_, sem, sems, counts, bank, x, contexts, w1_s, w2_s, wo_s, rw_s, ident, mod_t, gates, w_in, out):
    with ExitStack() as own:
        def sb(name, shape, dt=F32):
            return sb_(name, shape, dt, own)

        num = [sb(f"num{p}", [P, KK, TB]) for p in range(2)]
        den = [sb(f"den{p}", [P, KK, TB]) for p in range(2)]
        xres = [sb(f"xres{p}", [P, TT, D]) for p in range(2)]
        gated = sb("gated", [P, TT, D])
        stats = sb("stats_b", [P, TT, 6])
        mv = sb("mv_b", [P, TT, 2])
        rstd = sb("rstd_b", [P, TT])
        xn = sb("xn_b", [P, TT, D])
        h2t = [sb(f"h2t{p}", [P, KK, TB]) for p in range(2)]
        gate_e = sb("gate_e", [P, TT, E])
        prob = sb("prob", [P, TT, E])
        rank = sb("rank", [P, TT, E])
        beats = sb("beats", [P, TT, E])
        top = sb("top", [P, TT, E])
        top_sum = sb("top_sum", [P, TT])
        combine = [sb(f"combine{p}", [P, TT, E]) for p in range(2)]
        relu = [sb(f"relu{k}", [P, TB]) for k in range(2)]
        hid = [sb(f"hid{k}", [P, TB]) for k in range(3)]
        mix = [sb(f"mix{p}", [P, TT, D]) for p in range(2)]
        res = [sb(f"res{p}", [P, TT, D]) for p in range(2)]

        ctx_in, x_in = sems("ctx_in"), sems("xres_in")
        ctx_norm = sems("ctx_norm")
        rooted, inverted = sems("rooted_b"), sems("inverted_b")
        o_mm, res_done, ln_steps = sems("o_mm"), sems("res_done"), sems("ln_steps")
        t_mm, h_done = sems("t2_mm"), sems("h2_done")
        r_mm, r_exp, r_steps = sems("r_mm"), sems("r_exp"), sems("r_steps")
        u_mm, relu_done, hid_done, d_mm = sems("u_mm"), sems("relu_done"), sems("hid_done"), sems("d_mm")
        mix_done, final, out_done = sems("mix_done"), sems("final"), sems("out_done")
        last = NBLK // 2 - 1
        RS = 3 + 2 * E + 5

        def batch(p, i):
            return (2 * i + p) // BPB if isinstance(i, int) else i // (BPB // 2)

        sp_passed, dve_passed = sem("sp_passed_b"), sem("dve_passed_b")
        count_from_first(nc, counts)
        with nc.Block() as block:
            @block.sync
            def _(sp):
                sp.wait_ge(w_in, 64)

                def load_contexts(p, i):
                    n = 2 * i + p
                    wait_apart(sp, o_mm[p], FIRST + TT * i, sp_passed)
                    cols = bass.ds(n * TB, TB)
                    for k in range(KK):
                        rows = contexts[k * H // KK * VW:(k + 1) * H // KK * VW, cols].rearrange(
                            "(h c) t -> h c t", c=VW)
                        sp.dma_start(num[p][:, k, :], rows[:, 0:DK, :]).then_inc(ctx_in[p], 16)
                        sp.dma_start(den[p][:, k, :], rows[:, DK:VW, :]).then_inc(ctx_in[p], 16)

                def load_x(p, i):
                    cols = bass.ds((2 * i + p) * TB, TB)
                    wait_apart(sp, final[p], FIRST + 2 * TT * i, sp_passed)
                    sp.dma_start(xres[p][:, :, :], x[cols, :].rearrange("(t p) d -> p t d", p=P)
                                 ).then_inc(x_in[p], 16)

                def store(p, i):
                    wait_apart(sp, final[p], FIRST + 2 * TT * (i + 1), sp_passed)
                    sp.dma_start(out[bass.ds((2 * i + p) * TB, TB), :].rearrange("(t p) d -> p t d", p=P),
                                 res[p][:, :, :]).then_inc(out_done[p], 16)

                for p in range(2):
                    load_contexts(p, 0)
                    load_x(p, 0)
                with sp.Fori(0, last) as i:
                    for p in range(2):
                        load_contexts(p, i + 1)
                        store(p, i)
                        load_x(p, i + 1)
                for p in range(2):
                    store(p, last)
                for p in range(2):
                    sp.wait_ge(out_done[p], FIRST + 16 * (last + 1))

            @block.gpsimd
            def _(pool):
                def step(p, i, b):
                    pool.wait_ge(out_done[p], FIRST + 16 * i)
                    pool.wait_ge(mix_done[p], FIRST + TT * E * (i + 1))
                    for t in range(TT):
                        nc.gpsimd.tensor_tensor(res[p][:, t, :], mix[p][:, t, :],
                                                gates[:, bass.ds(b, 1), D:2 * D].squeeze(1), ALU.mult
                                                ).then_inc(final[p], 1)
                    for t in range(TT):
                        pool.wait_ge(final[p], FIRST + 2 * TT * i + t + 1)
                        nc.gpsimd.tensor_tensor(res[p][:, t, :], res[p][:, t, :], xres[p][:, t, :], ALU.add
                                                ).then_inc(final[p], 1)

                with pool.Fori(0, last + 1) as i:
                    for p in range(2):
                        step(p, i, batch(p, i))

            @block.scalar
            def _(act):
                def router_exp(p, i):
                    act.wait_ge(r_mm[p], FIRST + i + 1)
                    act.wait_ge(r_steps[1 - p], FIRST + RS * (i + p))
                    nc.scalar.activation(gate_e[:, :, :], bank(6)[:, 0:TT * E].rearrange("p (t e) -> p t e", e=E),
                                         ACT.Exp, scale=-1.0).then_inc(r_exp[p], 1)

                def root(p, i):
                    act.wait_ge(ln_steps[p], FIRST + (4 * TT + 1) * (i + 1))
                    nc.scalar.activation(rstd[:, :], rstd[:, :], ACT.Sqrt).then_inc(rooted[p], 1)

                def step(p, i, more=True):
                    for w in range(NW):
                        act.wait_ge(u_mm[p], FIRST + NW * i + w + 1)
                        if w >= 2:
                            act.wait_ge(hid_done[p], FIRST + NW * i + w - 1)
                        elif w == 0:
                            act.wait_ge(hid_done[1 - p], FIRST + NW * (i + p))
                        nc.scalar.activation(relu[w % 2][:, :], bank(w % 2), ACT.Relu).then_inc(relu_done[p], 1)
                        if w == 8 and more:
                            root(*following(p, i))
                        if w == 16 and more:
                            router_exp(*following(p, i))

                root(0, 0)
                router_exp(0, 0)
                with act.Fori(0, last) as i:
                    for p in range(2):
                        step(p, i)
                step(0, last)
                step(1, last, more=False)

            @block.vector
            def _(dve):
                def contexts_over_denominators(p, i):
                    dve.wait_ge(ctx_in[p], FIRST + 64 * (i + 1))
                    nc.vector.reciprocal(den[p][:, :, :], den[p][:, :, :]).then_inc(ctx_norm[p], 1)
                    dve.wait_ge(ctx_norm[p], FIRST + 2 * i + 1)
                    nc.vector.tensor_tensor(num[p][:, :, :], num[p][:, :, :], den[p][:, :, :], ALU.mult
                                            ).then_inc(ctx_norm[p], 1)

                def residual(p, i, b):
                    dve.wait_ge(x_in[p], FIRST + 16 * (i + 1))
                    dve.wait_ge(t_mm[1 - p], FIRST + KK * (i + p))
                    n = 4 * TT + 1
                    for t in range(TT):
                        dve.wait_ge(o_mm[p], FIRST + TT * i + 2 * (t // 2) + 2)
                        nc.vector.tensor_tensor(gated[:, t, :], bank(6 + t // 2)[:, (t % 2) * D:(t % 2 + 1) * D],
                                                gates[:, bass.ds(b, 1), 0:D].squeeze(1), ALU.mult
                                                ).then_inc(ln_steps[p], 1)
                    for t in range(TT):
                        dve.wait_ge(ln_steps[p], FIRST + n * i + t + 1)
                        nc.vector.tensor_tensor(xres[p][:, t, :], gated[:, t, :], xres[p][:, t, :], ALU.add
                                                ).then_inc(ln_steps[p], 1)
                    for t in range(TT):
                        dve.wait_ge(ln_steps[p], FIRST + n * i + TT + t + 1)
                        nc.vector.bn_stats(stats[:, t, :], xres[p][:, t, :]).then_inc(ln_steps[p], 1)
                    for t in range(TT):
                        wait_apart(dve, ln_steps[p], FIRST + n * i + 2 * TT + t + 1, dve_passed)
                        nc.vector.bn_aggr(mv[:, t, :], stats[:, t, :]).then_inc(ln_steps[p], 1)
                    dve.wait_ge(ln_steps[p], FIRST + n * i + 4 * TT)
                    nc.vector.tensor_scalar(rstd[:, :], mv[:, :, 1], EPS, None, ALU.add
                                            ).then_inc(ln_steps[p], 1)

                def normalise(p, i):
                    dve.wait_ge(rooted[p], FIRST + i + 1)
                    nc.vector.reciprocal(rstd[:, :], rstd[:, :]).then_inc(inverted[p], 1)
                    dve.wait_ge(inverted[p], FIRST + i + 1)
                    for t in range(TT):
                        nc.vector.tensor_scalar(xn[:, t, :], xres[p][:, t, :], mv[:, t, 0:1], rstd[:, t:t + 1],
                                                ALU.subtract, ALU.mult).then_inc(res_done[p], 1)

                def modulate(p, i, b):
                    dve.wait_ge(u_mm[p], FIRST + NW * i)
                    for k in range(KK):
                        dve.wait_ge(t_mm[p], FIRST + KK * i + k + 1)
                        nc.vector.tensor_scalar(h2t[p][:, k, :], bank(6 + k), mod_t[:, 3, k, bass.ds(b, 1)],
                                                mod_t[:, 2, k, bass.ds(b, 1)], ALU.mult, ALU.add
                                                ).then_inc(h_done[p], 1)

                def router(p, i):
                    n = [RS * i]

                    def linked(ins):
                        ins.then_inc(r_steps[p], 1)
                        n[0] = n[0] + 1
                        dve.wait_ge(r_steps[p], FIRST + n[0])

                    dve.wait_ge(r_exp[p], FIRST + i + 1)
                    dve.wait_ge(mix_done[p], FIRST + TT * E * i)
                    linked(nc.vector.tensor_scalar(gate_e[:, :, :], gate_e[:, :, :], 1.0, None, ALU.add))
                    linked(nc.vector.reciprocal(prob[:, :, :], gate_e[:, :, :]))
                    linked(nc.vector.memset(rank[:, :, :], 0.0))
                    for e in range(E):
                        one = prob[:, :, e:e + 1]
                        nc.vector.tensor_tensor(beats[:, :, 0:e + 1], one.to_broadcast([P, TT, e + 1]),
                                                prob[:, :, 0:e + 1], ALU.is_gt)
                        if e + 1 < E:
                            nc.vector.tensor_tensor(beats[:, :, e + 1:E], one.to_broadcast([P, TT, E - e - 1]),
                                                    prob[:, :, e + 1:E], ALU.is_ge).then_inc(r_steps[p], 1)
                        else:
                            nc.vector.engine_nop().then_inc(r_steps[p], 1)
                        n[0] = n[0] + 1
                        dve.wait_ge(r_steps[p], FIRST + n[0])
                        linked(nc.vector.tensor_tensor(rank[:, :, :], rank[:, :, :], beats[:, :, :], ALU.add))
                    linked(nc.vector.scalar_tensor_tensor(out=top[:, :, :], in0=rank[:, :, :], scalar=2.0,
                                                          in1=prob[:, :, :], op0=ALU.is_lt, op1=ALU.mult))
                    linked(nc.vector.tensor_reduce(top_sum[:, :], top[:, :, :], AX.X, ALU.add))
                    linked(nc.vector.tensor_scalar(top_sum[:, :], top_sum[:, :], 1e-20, None, ALU.add))
                    linked(nc.vector.reciprocal(top_sum[:, :], top_sum[:, :]))
                    linked(nc.vector.tensor_tensor(combine[p][:, :, :], top[:, :, :],
                                                   top_sum[:, :].unsqueeze(2).to_broadcast([P, TT, E]), ALU.mult))

                def hidden(p, i, w):
                    dve.wait_ge(relu_done[p], FIRST + NW * i + w + 1)
                    if w >= 3:
                        dve.wait_ge(d_mm[p], FIRST + NW * i + w - 2)
                    elif w == 0:
                        dve.wait_ge(d_mm[1 - p], FIRST + NW * (i + p))
                    nc.vector.tensor_tensor(hid[w % 3][:, :], bank(w % 2), relu[w % 2][:, :], ALU.mult
                                            ).then_inc(hid_done[p], 1)

                def mixed(p, i, e):
                    dve.wait_ge(d_mm[p], FIRST + NW * i + FIRST_W[e] + FT[e])
                    if e == 0:
                        dve.wait_ge(final[p], FIRST + 2 * TT * i)
                    for t in range(TT):
                        y = bank(2 + 2 * (e % 2) + t // 2)[:, (t % 2) * D:(t % 2 + 1) * D]
                        share = combine[p][:, t, e:e + 1]
                        if e == 0:
                            nc.vector.tensor_scalar(mix[p][:, t, :], y, share, None, ALU.mult
                                                    ).then_inc(mix_done[p], 1)
                        else:
                            dve.wait_ge(mix_done[p], FIRST + TT * E * i + TT * (e - 1) + t + 1)
                            nc.vector.scalar_tensor_tensor(out=mix[p][:, t, :], in0=y, scalar=share,
                                                           in1=mix[p][:, t, :], op0=ALU.mult, op1=ALU.add
                                                           ).then_inc(mix_done[p], 1)

                def step(p, i, more=True):
                    nxt = following(p, i)
                    b = batch(*nxt)
                    for w in range(NW):
                        hidden(p, i, w)
                        if more and w == 2:
                            contexts_over_denominators(*nxt)
                        if more and w == 7:
                            residual(*nxt, b)
                        if more and w == 9:
                            normalise(*nxt)
                        if more and w == 13:
                            modulate(*nxt, b)
                        if more and w == 18:
                            router(*nxt)
                        if w >= 2 and EXPERT[w - 2] != EXPERT[w - 1]:
                            mixed(p, i, EXPERT[w - 2])
                    mixed(p, i, E - 1)

                contexts_over_denominators(0, 0)
                residual(0, 0, 0)
                normalise(0, 0)
                modulate(0, 0, 0)
                router(0, 0)
                with dve.Fori(0, last) as i:
                    for p in range(2):
                        step(p, i)
                step(0, last)
                step(1, last, more=False)

            @block.tensor
            def _(pe):
                pe.wait_ge(w_in, 64)

                def project(p, i):
                    pe.wait_ge(ctx_norm[p], FIRST + 2 * (i + 1))
                    pe.wait_ge(r_exp[1 - p], FIRST + i + p)
                    for t in range(TT):
                        o = bank(6 + t // 2)[:, (t % 2) * D:(t % 2 + 1) * D]
                        for k in range(KK):
                            mm = nc.tensor.matmul(o, num[p][:, k, t * P:(t + 1) * P], wo_s[:, k, :],
                                                  start=(k == 0), stop=(k == KK - 1))
                        mm.then_inc(o_mm[p], 1)

                def transposes(p, i):
                    pe.wait_ge(res_done[p], FIRST + TT * (i + 1))
                    for k in range(KK):
                        for t in range(TT):
                            mm = nc.tensor.transpose(bank(6 + k)[:, t * P:(t + 1) * P],
                                                     xn[:, t, k * P:(k + 1) * P], ident[:, :])
                        mm.then_inc(t_mm[p], 1)

                def route(p, i):
                    pe.wait_ge(h_done[p], FIRST + KK * (i + 1))
                    for t in range(TT):
                        for k in range(KK):
                            mm = nc.tensor.matmul(bank(6)[:, t * E:(t + 1) * E], h2t[p][:, k, t * P:(t + 1) * P],
                                                  rw_s[:, k, :], start=(k == 0), stop=(k == KK - 1))
                    mm.then_inc(r_mm[p], 1)

                def up(p, i, w):
                    if w == 0:
                        pe.wait_ge(h_done[p], FIRST + KK * (i + 1))
                        pe.wait_ge(hid_done[1 - p], FIRST + NW * (i + p))
                    elif w >= 2:
                        pe.wait_ge(hid_done[p], FIRST + NW * i + w - 1)
                    for k in range(KK):
                        mm = nc.tensor.matmul(bank(w % 2), w1_s[:, k, w * P:(w + 1) * P], h2t[p][:, k, :],
                                              start=(k == 0), stop=(k == KK - 1))
                    mm.then_inc(u_mm[p], 1)

                def down(p, i, w):
                    e = EXPERT[w]
                    pe.wait_ge(hid_done[p], FIRST + NW * i + w + 1)
                    if w == FIRST_W[e]:
                        if e >= 2:
                            pe.wait_ge(mix_done[p], FIRST + TT * (E * i + e - 1))
                        else:
                            pe.wait_ge(mix_done[1 - p], FIRST + TT * E * (i + p))
                    for t in range(TT):
                        y = bank(2 + 2 * (e % 2) + t // 2)[:, (t % 2) * D:(t % 2 + 1) * D]
                        mm = nc.tensor.matmul(y, hid[w % 3][:, t * P:(t + 1) * P], w2_s[:, w, :],
                                              start=(w == FIRST_W[e] and t % 2 == 0),
                                              stop=(w == FIRST_W[e] + FT[e] - 1), skip_group_check=True)
                    mm.then_inc(d_mm[p], 1)

                def step(p, i, more=True):
                    nxt = following(p, i)
                    up(p, i, 0)
                    up(p, i, 1)
                    for w in range(NW):
                        down(p, i, w)
                        if w + 2 < NW:
                            up(p, i, w + 2)
                        if more and w == 5:
                            project(*nxt)
                        if more and w == 11:
                            transposes(*nxt)
                        if more and w == 14:
                            route(*nxt)

                project(0, 0)
                transposes(0, 0)
                route(0, 0)
                with pe.Fori(0, last) as i:
                    for p in range(2):
                        step(p, i)
                step(0, last)
                step(1, last, more=False)


def kernel(L0_attn_x, L0_attn_W_qkv, L0_attn_W_o, L0_ffn_router_w, L0_ffn_w1, L0_ffn_w2, L0_c, L0_wmod):
    import numpy as np
    import concourse.bacc as bacc
    from concourse.bass_utils import run_bass_kernel_spmd

    laid = {
        "x": np.asarray(L0_attn_x).reshape(T, D),
        "wqkv_t": np.asarray(L0_attn_W_qkv).reshape(3 * D, D).T,
        "wo_t": np.asarray(L0_attn_W_o).T,
        "rw_t": np.asarray(L0_ffn_router_w).T,
        "w1": np.asarray(L0_ffn_w1),
        "w2": np.asarray(L0_ffn_w2),
        "c_t": np.asarray(L0_c).T,
        "wmod": np.asarray(L0_wmod),
    }
    nc = bacc.Bacc("TRN2", target_bir_lowering=False, num_devices=1)
    nc.disable_value_cache = True
    arrays, args = {}, []
    for name, a in laid.items():
        arrays[f"in_{name}"] = np.ascontiguousarray(a)
        args.append(nc.dram_tensor(f"in_{name}", a.shape, F32, kind="ExternalInput").ap())
    args.append(nc.dram_tensor("out_0", (T, D), F32, kind="ExternalOutput").ap())
    adaln_layer(nc, *args)
    r = run_bass_kernel_spmd(nc, [arrays], core_ids=[0])
    return r.results[0]["out_0"].reshape(B, S, D)
```

```python
from contextlib import ExitStack

import concourse.bass as bass
from concourse import mybir

F32 = mybir.dt.float32
F32R = mybir.dt.float32r
BF16 = mybir.dt.bfloat16
ALU = mybir.AluOpType
ACT = mybir.ActivationFunctionType
AX = mybir.AxisListType

P = 128
B, S, D, H = 4, 2048, 256, 16
DK = D // H
T = B * S
KK = D // P
TB = 512
TT = TB // P
NBLK = T // TB
BPB = S // TB
SCALE = DK ** -0.5
EPS = 1e-5
NEG = -1e30

HG = 4
NG = B * H // HG
QT = S // P
PARTS = 3
STACK = 6 * DK
VW = 2 * DK

WIDTHS = [256] * 4 + [512] * 4
E = len(WIDTHS)
FT = [w // P for w in WIDTHS]
NW = sum(FT)
EXPERT = [e for e in range(E) for _ in range(FT[e])]
FIRST_W = [sum(FT[:e]) for e in range(E)]

UNITS = [(j, kt, max(0, kt - TT * j) * P) for j in range(BPB) for kt in range(TT * (j + 1))]
NU = len(UNITS)
NS = HG * NU
DIAG = [kt >= TT * j for j, kt, _ in UNITS]
UNITS_TO = [TT * (j + 1) * (j + 2) // 2 for j in range(BPB)]
FIRST = 1
LAG = 2
POOL_LO = [w for w in range(NW) if w % 3 == 1]
HB = 3
SB = 3
PB = 4

CW = 512
MS = 4
CHUNKS = [
    (h, t, k0, min(CW, P * (t + 1) - k0), k0 + CW >= P * (t + 1))
    for h in range(HG) for t in range(QT) for k0 in range(0, P * (t + 1), CW)
]
NC = len(CHUNKS)


def chunk_plan():
    steps = [(n, k) for n in range(PLAN_FIRST, PLAN_LAST) for k in range(POINTS)]
    main_cost = [TB - q0 + STEP_COST for _, _, q0 in UNITS]
    chunk_cost = [w + STEP_COST for *_, w, _ in CHUNKS]
    span, total = sum(main_cost[n] for n, _ in steps), sum(chunk_cost)
    plan, c, done, spent = [[] for _ in range(POINTS * NU)], 0, 0, 0
    for n, k in steps:
        spent += main_cost[n]
        while c < NC and done * span < spent * total:
            plan[POINTS * n + k].append(c)
            done += chunk_cost[c]
            c += 1
    return plan


STEP_COST = 64
POINTS = 5
PLAN_FIRST, PLAN_LAST = 3, NU - 4
PLAN = chunk_plan()


def count_from_first(nc, counts):
    with nc.Block() as block:
        @block.sync
        def _(sp):
            for s in counts[0::4]:
                sp.sem_inc(s, FIRST)

        @block.scalar
        def _(act):
            for s in counts[1::4]:
                act.sem_inc(s, FIRST)

        @block.vector
        def _(dve):
            for s in counts[2::4]:
                dve.sem_inc(s, FIRST)

        @block.gpsimd
        def _(pool):
            for s in counts[3::4]:
                pool.sem_inc(s, FIRST)

    counts.clear()


def wait_apart(engine, semaphore, value, passed):
    engine.wait_ge(semaphore, value)
    engine.sem_inc(passed, 1)


def following(p, i):
    return 1 - p, i + p


def adaln_layer(nc, x, wqkv_t, wo_t, rw_t, w1, w2, c_t, wmod, out):
    q_parts = nc.dram_tensor("q_parts", (D, PARTS, T), BF16, kind="Internal").ap()
    k_parts = nc.dram_tensor("k_parts", (D, PARTS, T), BF16, kind="Internal").ap()
    v_ones = nc.dram_tensor("v_ones", (T, H * VW), F32, kind="Internal").ap()
    contexts = nc.dram_tensor("contexts", (H * VW, T), F32, kind="Internal").ap()

    with ExitStack() as whole:
        def sb(name, shape, dt=F32, at=whole):
            return at.enter_context(nc.sbuf_tensor(name, shape, dt))

        def sem(name):
            return whole.enter_context(nc.semaphore(name))

        counts = []

        def sems(name, n=2):
            made = [sem(f"{name}{k}") for k in range(n)]
            counts.extend(made)
            return made

        ps = whole.enter_context(nc.psum_tensor("ps", [P, 8 * 512], F32))

        def bank(n, count=1):
            return ps[:, n * 512:(n + count) * 512]

        wo_s = sb("wo_s", [P, KK, D])
        rw_s = sb("rw_s", [P, KK, E])
        ident = sb("ident", [P, P])
        mod_t = sb("mod_t", [P, 4, KK, B])
        gates = sb("gates", [P, B, 2 * D])

        w_in = sem("w_in")
        block1(nc, sb, sem, sems, counts, bank, x, wqkv_t, wo_t, rw_t, c_t, wmod, q_parts, k_parts, v_ones,
               wo_s, rw_s, ident, mod_t, gates, w_in)
        block2(nc, sb, sem, sems, counts, bank, q_parts, k_parts, v_ones, contexts, ident)
        block3(nc, sb, sem, sems, counts, bank, x, contexts, w1, w2, wo_s, rw_s, ident, mod_t, gates, w_in, out)


def preceding(p, i):
    return 1 - p, i + p - 1


def block1(nc, sb_, sem, sems, counts, bank, x, wqkv_t, wo_t, rw_t, c_t, wmod, q_parts, k_parts, v_ones,
           wo_s, rw_s, ident, mod_t, gates, w_in):
    with ExitStack() as own:
        def sb(name, shape, dt=F32):
            return sb_(name, shape, dt, own)

        wqkv_s = sb("wqkv_s", [P, KK, 3 * D])
        wmod_s = sb("wmod_s", [P, KK, 6 * D])
        ct = sb("ct", [P, KK, B])
        ce = sb("ce", [P, KK, B])
        silu = sb("silu", [P, KK, B])
        silu_all = sb("silu_all", [P, KK, B, P])
        sign = sb("sign", [P, B, 2 * D])
        size = sb("size", [P, B, 2 * D])
        xin = [sb(f"xin{p}", [P, TT, D]) for p in range(2)]
        stats = [sb(f"stats{p}", [P, TT, 6]) for p in range(2)]
        mv = [sb(f"mv{p}", [P, TT, 2]) for p in range(2)]
        rstd = [sb(f"rstd{p}", [P, TT]) for p in range(2)]
        xn = [sb(f"xn{p}", [P, TT, D]) for p in range(2)]
        ht = [sb(f"ht{p}", [P, KK, TB]) for p in range(2)]
        rest = sb("rest", [P, 4, TB])
        parts = [sb(f"parts{p}", [P, 4, PARTS, TB], BF16) for p in range(2)]
        vt = [sb(f"vt{p}", [P, TT, H, VW]) for p in range(2)]

        setup_in = sem("setup_in")
        id_zero, id_done = sem("id_zero"), sem("id_done")
        c_steps, c_exp = sem("c_steps"), sem("c_exp")
        mod_mm, gate_mm = sem("mod_mm"), sem("gate_mm")
        gate_steps = sem("gate_steps")
        ones_set = sem("ones_set")
        x_in, stat_done, xn_done = sems("x_in"), sems("stat_done"), sems("xn_done")
        rooted, inverted = sems("rooted"), sems("inverted")
        t_mm, ht_done = sems("t_mm"), sems("ht_done")
        qk_mm, part1, rest1, part2, part3 = (sems(n) for n in ("qk_mm", "part1_", "rest1_", "part2_", "part3_"))
        v_mm, v_done = sems("v_mm"), sems("v_done")
        stored = sems("stored")

        sp_passed, dve_passed = sem("sp_passed"), sem("dve_passed")
        count_from_first(nc, counts)
        with nc.Block() as block:
            @block.sync
            def _(sp):
                sp.dma_start(ct[:, :, :], c_t.rearrange("(k p) b -> p k b", p=P)).then_inc(setup_in, 16)
                sp.dma_start(wmod_s[:, :, :], wmod.rearrange("(k p) n -> p k n", p=P)).then_inc(setup_in, 16)
                sp.dma_start(wqkv_s[:, :, :], wqkv_t.rearrange("(k p) n -> p k n", p=P)).then_inc(setup_in, 16)

                def store(p, i):
                    cols = bass.ds((2 * i + p) * TB, TB)
                    for o in range(4):
                        to = (q_parts, k_parts)[o // 2]
                        wait_apart(sp, part3[p], FIRST + 4 * i + o + 1, sp_passed)
                        sp.dma_start(to[P * (o % 2):P * (o % 2 + 1), :, cols],
                                     parts[p][:, o, :, :]).then_inc(stored[p], 16)
                    wait_apart(sp, v_done[p], FIRST + 2 * (i + 1), sp_passed)
                    sp.dma_start(v_ones[cols, :].rearrange("(t p) c -> p t c", p=P),
                                 vt[p][:, :, :, :].rearrange("p t h c -> p t (h c)")).then_inc(stored[p], 16)

                sp.dma_start(wo_s[:, :, :], wo_t.rearrange("(k p) n -> p k n", p=P)).then_inc(w_in, 16)
                sp.dma_start(rw_s[:, :, :], rw_t.rearrange("(k p) n -> p k n", p=P)).then_inc(w_in, 16)
                with sp.Fori(0, NBLK // 2) as i:
                    for p in range(2):
                        store(p, i)
                for p in range(2):
                    sp.wait_ge(stored[p], FIRST + 16 * 5 * NBLK // 2)

            @block.gpsimd
            def _(pool):
                nc.gpsimd.memset(ident[:, :], 0.0).then_inc(id_zero, 1)
                pool.wait_ge(id_zero, 1)
                nc.gpsimd.affine_select(out=ident[:, :], in_=ident[:, :], compare_op=ALU.not_equal, fill=1.0,
                                        base=0, pattern=[[-1, P]], channel_multiplier=1).then_inc(id_done, 1)
                for p in range(2):
                    nc.gpsimd.memset(vt[p][:, :, :, DK:VW], 1.0).then_inc(ones_set, 1)

            @block.scalar
            def _(act):
                def load(p, i):
                    act.wait_ge(xn_done[p], FIRST + TT * i)
                    src = x[bass.ds((2 * i + p) * TB, TB), :].rearrange("(t p) d -> p t d", p=P)
                    act.dma_start(xin[p][:, :, :], src).then_inc(x_in[p], 16)

                load(0, 0)
                load(1, 0)
                act.wait_ge(setup_in, 48)
                nc.scalar.activation(ce[:, :, :], ct[:, :, :], ACT.Exp, scale=-1.0).then_inc(c_exp, 1)
                act.wait_ge(ones_set, 2)

                def part_1(p, i, o):
                    act.wait_ge(qk_mm[p], FIRST + 4 * i + o + 1)
                    if o == 0:
                        act.wait_ge(stored[p], FIRST + 80 * i)
                    nc.scalar.activation(parts[p][:, o, 0, :], bank(2 + o), ACT.Copy).then_inc(part1[p], 1)

                def part_2(p, i, o):
                    act.wait_ge(rest1[p], FIRST + 4 * i + o + 1)
                    nc.scalar.activation(parts[p][:, o, 1, :], rest[:, o, :], ACT.Copy).then_inc(part2[p], 1)

                def values(p, i, half):
                    act.wait_ge(v_mm[p], FIRST + 2 * i + half + 1)
                    nc.scalar.activation(
                        vt[p][:, 2 * half:2 * half + 2, :, 0:DK],
                        bank(6 + half).rearrange("p (t h c) -> p t h c", t=2, h=H), ACT.Copy).then_inc(v_done[p], 1)

                def root(p, i):
                    act.wait_ge(stat_done[p], FIRST + 9 * (i + 1))
                    nc.scalar.activation(rstd[p][:, :], rstd[p][:, :], ACT.Sqrt).then_inc(rooted[p], 1)

                def step(p, i, more=True, loads=True):
                    if loads:
                        load(p, i + 1)
                    part_1(p, i, 0)
                    for o in range(1, 4):
                        part_1(p, i, o)
                        part_2(p, i, o - 1)
                        if o == 1 and more:
                            root(*following(p, i))
                    part_2(p, i, 3)
                    for half in range(2):
                        values(p, i, half)

                root(0, 0)
                last = NBLK // 2 - 1
                with act.Fori(0, last) as i:
                    for p in range(2):
                        step(p, i)
                step(0, last, loads=False)
                step(1, last, more=False, loads=False)

            @block.vector
            def _(dve):
                dve.wait_ge(c_exp, 1)
                nc.vector.tensor_scalar(ce[:, :, :], ce[:, :, :], 1.0, None, ALU.add).then_inc(c_steps, 1)
                dve.wait_ge(c_steps, 1)
                nc.vector.reciprocal(ce[:, :, :], ce[:, :, :]).then_inc(c_steps, 1)
                dve.wait_ge(c_steps, 2)
                nc.vector.tensor_tensor(silu[:, :, :], ct[:, :, :], ce[:, :, :], ALU.mult).then_inc(c_steps, 1)
                dve.wait_ge(c_steps, 3)
                nc.vector.tensor_copy(silu_all[:, :, :, :], silu[:, :, :].unsqueeze(3).to_broadcast([P, KK, B, P])
                                      ).then_inc(c_steps, 1)

                def gate_guard():
                    dve.wait_ge(gate_mm, 1)
                    g = bank(0, B).rearrange("p (b n) -> p b n", b=B)
                    nc.vector.tensor_scalar(sign[:, :, :], g, 0.0, 2.0, ALU.is_ge, ALU.mult).then_inc(gate_steps, 1)
                    dve.wait_ge(gate_steps, 1)
                    nc.vector.scalar_tensor_tensor(out=size[:, :, :], in0=sign[:, :, :], scalar=1.0, in1=g,
                                                   op0=ALU.subtract, op1=ALU.mult).then_inc(gate_steps, 1)
                    dve.wait_ge(gate_steps, 2)
                    nc.vector.tensor_scalar(size[:, :, :], size[:, :, :], 0.25, None, ALU.max
                                            ).then_inc(gate_steps, 1)
                    dve.wait_ge(gate_steps, 3)
                    nc.vector.scalar_tensor_tensor(out=gates[:, :, :], in0=sign[:, :, :], scalar=1.0,
                                                   in1=size[:, :, :], op0=ALU.subtract, op1=ALU.mult
                                                   ).then_inc(gate_steps, 1)
                    dve.wait_ge(mod_mm, 1)
                    m = bank(4)[:, 0:4 * KK * B].rearrange("p (w k b) -> p w k b", w=4, k=KK)
                    for w in range(4):
                        nc.vector.tensor_scalar(mod_t[:, w], m[:, w], float(w % 2), None, ALU.add
                                                ).then_inc(gate_steps, 1)
                    dve.wait_ge(gate_steps, 8)

                def variance(p, i):
                    dve.wait_ge(x_in[p], FIRST + 16 * (i + 1))
                    for t in range(TT):
                        nc.vector.bn_stats(stats[p][:, t, :], xin[p][:, t, :]).then_inc(stat_done[p], 1)
                    for t in range(TT):
                        wait_apart(dve, stat_done[p], FIRST + 9 * i + t + 1, dve_passed)
                        nc.vector.bn_aggr(mv[p][:, t, :], stats[p][:, t, :]).then_inc(stat_done[p], 1)
                    dve.wait_ge(stat_done[p], FIRST + 9 * i + 8)
                    nc.vector.tensor_scalar(rstd[p][:, :], mv[p][:, :, 1], EPS, None, ALU.add
                                            ).then_inc(stat_done[p], 1)

                def normalise(p, i):
                    dve.wait_ge(rooted[p], FIRST + i + 1)
                    nc.vector.reciprocal(rstd[p][:, :], rstd[p][:, :]).then_inc(inverted[p], 1)
                    dve.wait_ge(inverted[p], FIRST + i + 1)
                    dve.wait_ge(t_mm[p], FIRST + 2 * i)
                    for t in range(TT):
                        nc.vector.tensor_scalar(xn[p][:, t, :], xin[p][:, t, :], mv[p][:, t, 0:1],
                                                rstd[p][:, t:t + 1], ALU.subtract, ALU.mult).then_inc(xn_done[p], 1)

                def modulate(p, i, b):
                    dve.wait_ge(v_mm[p], FIRST + 2 * i)
                    for k in range(KK):
                        dve.wait_ge(t_mm[p], FIRST + 2 * i + k + 1)
                        nc.vector.tensor_scalar(ht[p][:, k, :], bank(k), mod_t[:, 1, k, bass.ds(b, 1)],
                                                mod_t[:, 0, k, bass.ds(b, 1)], ALU.mult, ALU.add
                                                ).then_inc(ht_done[p], 1)

                def rest_1(p, i, o):
                    dve.wait_ge(part1[p], FIRST + 4 * i + o + 1)
                    dve.wait_ge(part3[1 - p], FIRST + 4 * (i + p))
                    nc.vector.tensor_tensor(rest[:, o, :], bank(2 + o), parts[p][:, o, 0, :], ALU.subtract
                                            ).then_inc(rest1[p], 1)

                def part_3(p, i, o):
                    dve.wait_ge(part2[p], FIRST + 4 * i + o + 1)
                    nc.vector.tensor_tensor(parts[p][:, o, 2, :], rest[:, o, :], parts[p][:, o, 1, :], ALU.subtract
                                            ).then_inc(part3[p], 1)

                def step(p, i, b, more=True):
                    rest_1(p, i, 0)
                    if more:
                        variance(*following(p, i))
                    rest_1(p, i, 1)
                    part_3(p, i, 0)
                    if more:
                        normalise(*following(p, i))
                    rest_1(p, i, 2)
                    part_3(p, i, 1)
                    rest_1(p, i, 3)
                    if more:
                        modulate(*following(p, i), b)
                    part_3(p, i, 2)
                    part_3(p, i, 3)

                variance(0, 0)
                gate_guard()
                normalise(0, 0)
                modulate(0, 0, 0)
                last = NBLK // 2 - 1
                with dve.Fori(0, last) as i:
                    for p in range(2):
                        step(p, i, (i + p) // (BPB // 2))
                step(0, last, B - 1)
                step(1, last, B - 1, more=False)

            @block.tensor
            def _(pe):
                pe.wait_ge(setup_in, 48)
                pe.wait_ge(id_done, 1)
                pe.wait_ge(c_steps, 4)
                for b in range(B):
                    for g, off in ((0, 2 * D), (1, 5 * D)):
                        for k in range(KK):
                            mm = nc.tensor.matmul(bank(b)[:, g * D:(g + 1) * D], silu_all[:, k, b, :],
                                                  wmod_s[:, k, off:off + D], start=(k == 0), stop=(k == KK - 1))
                mm.then_inc(gate_mm, 1)
                for w, which in enumerate((0, 1, 3, 4)):
                    for half in range(KK):
                        for k in range(KK):
                            c0 = which * D + half * P
                            n0 = (w * KK + half) * B
                            mm = nc.tensor.matmul(bank(4)[:, n0:n0 + B], wmod_s[:, k, c0:c0 + P],
                                                  silu[:, k, :], start=(k == 0), stop=(k == KK - 1))
                mm.then_inc(mod_mm, 1)
                pe.wait_ge(gate_steps, 8)

                def transposes(p, i):
                    pe.wait_ge(ht_done[1 - p], FIRST + 2 * (i + p))
                    pe.wait_ge(xn_done[p], FIRST + TT * (i + 1))
                    for k in range(KK):
                        for t in range(TT):
                            mm = nc.tensor.transpose(bank(k)[:, t * P:(t + 1) * P],
                                                     xn[p][:, t, k * P:(k + 1) * P], ident[:, :])
                        mm.then_inc(t_mm[p], 1)

                def queries_keys(p, i):
                    pe.wait_ge(ht_done[p], FIRST + KK * (i + 1))
                    for o in range(4):
                        pe.wait_ge(rest1[1 - p], FIRST + 4 * (i + p))
                        for k in range(KK):
                            mm = nc.tensor.matmul(bank(2 + o), wqkv_s[:, k, o * P:(o + 1) * P], ht[p][:, k, :],
                                                  start=(k == 0), stop=(k == KK - 1))
                        mm.then_inc(qk_mm[p], 1)

                def values(p, i):
                    pe.wait_ge(v_done[1 - p], FIRST + 2 * (i + p))
                    for t in range(TT):
                        o = bank(6 + t // 2)[:, (t % 2) * D:(t % 2 + 1) * D]
                        for k in range(KK):
                            mm = nc.tensor.matmul(o, ht[p][:, k, t * P:(t + 1) * P], wqkv_s[:, k, 2 * D:3 * D],
                                                  start=(k == 0), stop=(k == KK - 1))
                        if t % 2:
                            mm.then_inc(v_mm[p], 1)

                def step(p, i, more=True):
                    queries_keys(p, i)
                    if more:
                        transposes(*following(p, i))
                    values(p, i)

                transposes(0, 0)
                last = NBLK // 2 - 1
                with pe.Fori(0, last) as i:
                    for p in range(2):
                        step(p, i)
                step(0, last)
                step(1, last, more=False)


def block2(nc, sb_, sem, sems, counts, bank, q_parts, k_parts, v_ones, contexts, ident):
    with ExitStack() as own:
        def sb(name, shape, dt=F32):
            return sb_(name, shape, dt, own)

        qs = [sb(f"qs{p}", [STACK + PARTS, HG, S], BF16) for p in range(2)]
        ks = [sb(f"ks{p}", [STACK + PARTS, HG, S], BF16) for p in range(2)]
        vs = [sb(f"vs{p}", [P, QT, HG, VW]) for p in range(2)]
        probs = [sb(f"probs{k}", [P, HG, TB]) for k in range(PB)]
        causal = sb("causal", [P, CW])
        causal_b = sb("causal_b", [P, P], BF16)
        ident_b = sb("ident_b", [P, P], BF16)
        junk = [sb(f"junk{k}", [P, CW], BF16) for k in range(2)]
        maxima = [sb(f"maxima{p}", [P, HG, QT]) for p in range(2)]
        early = sb("early", [P, HG, QT, (S - 1) // CW])
        early_max = sb("early_max", [P, HG, QT])
        neg = [sb(f"neg{p}", [HG * QT, PARTS, P], BF16) for p in range(2)]
        neg_rest = sb("neg_rest", [HG * QT, P])
        ctx_out = [sb(f"ctx_out{k}", [P, TB]) for k in range(2)]

        causal_set = sem("causal_set")
        mask_set = sem("mask_set")
        ones_set = sem("k_ones_set")
        heads_in = [sems(f"heads_in{p}_", HG) for p in range(2)]
        v_in = sems("v_in")
        max_mm, max_done = sems("max_mm"), sems("max_done")
        joined = sems("joined")
        max_all, max_t = sems("max_all"), sems("max_t")
        neg_done, neg_in = sems("neg_done"), sems("neg_in")
        s_mm, exp_done = sems("s_mm"), sems("exp_done")
        pv_mm, ctx_done = sems("pv_mm"), sems("ctx_done")
        ctx_stored = sems("ctx_stored")
        last = NG // 2 - 1

        def place(p, i):
            per = B * H // HG // B
            return (2 * i + p) // per if isinstance(i, int) else i // (per // 2), (i % (per // 2)) * 2 + p

        sp_passed, dve_passed, pe_passed = (sem(f"{n}_passed_a") for n in ("sp", "dve", "pe"))
        count_from_first(nc, counts)
        with nc.Block() as block:
            @block.sync
            def _(sp):
                def load(p, i):
                    b, hg = place(p, i)
                    wait_apart(sp, s_mm[p], FIRST + NS * i, sp_passed)
                    for h in range(HG):
                        rows = bass.ds((hg * HG + h) * DK, DK)
                        toks = bass.ds(b * S, S)
                        for side, src, same in ((qs[p], q_parts, False), (ks[p], k_parts, True)):
                            for r0, n, other in ((0, 3, 0), (3 * DK, 2, 1), (5 * DK, 1, 2)):
                                if same:
                                    s = src[rows, other:other + 1, toks].to_broadcast([DK, n, S])
                                else:
                                    s = src[rows, 0:n, toks]
                                sp.dma_start(side[r0:r0 + n * DK, h, :], s).then_inc(heads_in[p][h], 16)

                def load_v(p, i):
                    b, hg = place(p, i)
                    wait_apart(sp, pv_mm[p], FIRST + NU * i, sp_passed)
                    src = v_ones[bass.ds(b * S, S), bass.ds(hg * (HG * VW), HG * VW)]
                    sp.dma_start(vs[p][:, :, :, :].rearrange("p t h c -> p t (h c)"),
                                 src.rearrange("(t p) c -> p t c", p=P)).then_inc(v_in[p], 16)

                def store(p, i, j):
                    b, hg = place(p, i)
                    wait_apart(sp, ctx_done[p], FIRST + BPB * i + j + 1, sp_passed)
                    sp.dma_start(contexts[bass.ds(hg * P, P), bass.ds(b * S + j * TB, TB)],
                                 ctx_out[j % 2][:, :]).then_inc(ctx_stored[j % 2], 16)

                def put_neg(p, i):
                    wait_apart(sp, neg_done[p], FIRST + 4 * (i + 1), sp_passed)
                    for n in range(PARTS):
                        sp.dma_start(qs[p][STACK + n:STACK + n + 1, :, :].rearrange("a h (t c) -> a (h t) c", c=P),
                                     neg[p][:, n, :]).then_inc(neg_in[p], 16)

                def step(p, i, before=True, more=True):
                    if more:
                        load(*following(p, i))
                    if before:
                        store(*preceding(p, i), BPB - 1)
                    if more:
                        load_v(*following(p, i))
                    for j in range(BPB - 1):
                        store(p, i, j)
                    if more:
                        put_neg(*following(p, i))

                load(0, 0)
                load_v(0, 0)
                put_neg(0, 0)
                step(0, 0, before=False)
                with sp.Fori(0, last) as i:
                    step(1, i)
                    step(0, i + 1)
                step(1, last, more=False)
                store(1, last, BPB - 1)
                for k in range(2):
                    sp.wait_ge(ctx_stored[k], FIRST + 16 * NG * BPB // 2)

            @block.gpsimd
            def _(pool):
                nc.gpsimd.memset(causal[:, :], 0.0).then_inc(causal_set, 1)
                pool.wait_ge(causal_set, 1)
                nc.gpsimd.affine_select(out=causal[:, CW - P:CW], in_=causal[:, CW - P:CW], compare_op=ALU.is_ge,
                                        fill=NEG, base=0, pattern=[[-1, P]], channel_multiplier=1
                                        ).then_inc(causal_set, 1)
                pool.wait_ge(causal_set, 2)
                for p in range(2):
                    pool.wait_ge(ones_set, p)
                    nc.gpsimd.memset(ks[p][STACK:STACK + PARTS, :, :], 1.0).then_inc(ones_set, 1)

            @block.scalar
            def _(act):
                def context(p, i, j):
                    act.wait_ge(pv_mm[p], FIRST + NU * i + UNITS_TO[j])
                    act.wait_ge(ctx_stored[j % 2], FIRST + 16 * (4 * i + 2 * p + j // 2))
                    nc.scalar.activation(ctx_out[j % 2][:, :], bank(3), ACT.Copy).then_inc(ctx_done[p], 1)

                def step(p, i, before=True):
                    for u, (j, kt, q0) in enumerate(UNITS):
                        if u >= PB:
                            act.wait_ge(pv_mm[p], FIRST + NU * i + u - PB + 1)
                        elif before:
                            act.wait_ge(pv_mm[1 - p], FIRST + NU * (i + p) + u - PB + 1)
                        for h in range(HG):
                            if h == 2 and u == LAG - 1 and before:
                                context(*preceding(p, i), BPB - 1)
                            if h == 2 and u - LAG + 1 in UNITS_TO:
                                context(p, i, UNITS_TO.index(u - LAG + 1))
                            n = HG * u + h
                            act.wait_ge(s_mm[p], FIRST + NS * i + n + 1)
                            nc.scalar.activation(probs[u % PB][:, h, q0:TB], bank(n % SB)[:, q0:TB], ACT.Exp,
                                                 scale=SCALE).then_inc(exp_done[p], 1)

                step(0, 0, before=False)
                with act.Fori(0, last) as i:
                    step(1, i)
                    step(0, i + 1)
                step(1, last)
                context(1, last, BPB - 1)

            @block.vector
            def _(dve):
                dve.wait_ge(causal_set, 2)
                nc.vector.memset(early[:, :, :, :], -3e38).then_inc(mask_set, 1)
                dve.wait_ge(mask_set, 1)
                nc.vector.tensor_copy(causal_b[:, :], causal[:, CW - P:CW]).then_inc(mask_set, 1)
                nc.vector.tensor_copy(ident_b[:, :], ident[:, :]).then_inc(mask_set, 1)

                def maxima_of(p, i):
                    for c, (h, t, k0, w, end) in enumerate(CHUNKS):
                        if c >= 2:
                            dve.wait_ge(max_done[p], FIRST + NC * i + c - 1)
                        wait_apart(dve, max_mm[p], FIRST + NC * i + c + 1, dve_passed)
                        tile = bank(4 + c % MS * (CW // 512), CW // 512)[:, 0:w]
                        if end:
                            nc.vector.tensor_tensor_reduce(
                                junk[c % 2][:, 0:w], tile, causal[:, CW - w:CW], 1.0, -3e38, ALU.add, ALU.max,
                                maxima[p][:, h, t:t + 1]).then_inc(max_done[p], 1)
                        else:
                            nc.vector.tensor_reduce(early[:, h, t, k0 // CW:k0 // CW + 1], tile, AX.X, ALU.max
                                                    ).then_inc(max_done[p], 1)
                    dve.wait_ge(max_done[p], FIRST + NC * (i + 1))
                    nc.vector.tensor_reduce(early_max[:, :, :], early[:, :, :, :], AX.X, ALU.max
                                            ).then_inc(joined[p], 1)
                    dve.wait_ge(joined[p], FIRST + i + 1)
                    nc.vector.tensor_tensor(maxima[p][:, :, :], maxima[p][:, :, :], early_max[:, :, :], ALU.max
                                            ).then_inc(max_all[p], 1)
                    dve.wait_ge(max_t[p], FIRST + i + 1)
                    dve.wait_ge(neg_in[p], FIRST + 48 * i)
                    m = bank(4)[0:HG * QT, 0:P]
                    nc.vector.tensor_scalar(neg[p][:, 0, :], m, -1.0, None, ALU.mult).then_inc(neg_done[p], 1)
                    dve.wait_ge(neg_done[p], FIRST + 4 * i + 1)
                    nc.vector.scalar_tensor_tensor(out=neg_rest[:, :], in0=m, scalar=-1.0, in1=neg[p][:, 0, :],
                                                   op0=ALU.mult, op1=ALU.subtract).then_inc(neg_done[p], 1)
                    dve.wait_ge(neg_done[p], FIRST + 4 * i + 2)
                    nc.vector.tensor_copy(neg[p][:, 1, :], neg_rest[:, :]).then_inc(neg_done[p], 1)
                    dve.wait_ge(neg_done[p], FIRST + 4 * i + 3)
                    nc.vector.tensor_tensor(neg[p][:, 2, :], neg_rest[:, :], neg[p][:, 1, :], ALU.subtract
                                            ).then_inc(neg_done[p], 1)

                maxima_of(0, 0)
                with dve.Fori(0, last) as i:
                    for p in range(2):
                        maxima_of(*following(p, i))
                maxima_of(1, last)

            @block.tensor
            def _(pe):
                pe.wait_ge(ones_set, 2)
                pe.wait_ge(mask_set, 3)

                def max_chunk(p, i, c):
                    h, t, k0, w, _ = CHUNKS[c]
                    if c == 0 or CHUNKS[c - 1][0] != h:
                        pe.wait_ge(heads_in[p][h], FIRST + 96 * (i + 1))
                    if c >= MS:
                        pe.wait_ge(max_done[p], FIRST + NC * i + c - MS + 1)
                    elif c == 0:
                        pe.wait_ge(neg_done[1 - p], FIRST + 4 * (i + p))
                    for m0 in range(0, w, 512):
                        n = min(512, w - m0)
                        mm = nc.tensor.matmul(bank(4 + c % MS * (CW // 512), CW // 512)[:, m0:m0 + n],
                                              qs[p][0:STACK, h, t * P:(t + 1) * P],
                                              ks[p][0:STACK, h, k0 + m0:k0 + m0 + n], start=True, stop=True)
                    mm.then_inc(max_mm[p], 1)

                def max_turn(p, i):
                    wait_apart(pe, max_all[p], FIRST + i + 1, pe_passed)
                    nc.tensor.transpose(bank(4)[0:HG * QT, 0:P], maxima[p][:, :, :].rearrange("p h t -> p (h t)"),
                                        ident[:, :]).then_inc(max_t[p], 1)

                def score(p, i, u, h):
                    j, kt, q0 = UNITS[u]
                    n = HG * u + h
                    if n == 0:
                        pe.wait_ge(neg_in[p], FIRST + 48 * (i + 1))
                        pe.wait_ge(exp_done[1 - p], FIRST + NS * (i + p))
                    elif n >= SB:
                        pe.wait_ge(exp_done[p], FIRST + NS * i + n - SB + 1)
                    mm = nc.tensor.matmul(bank(n % SB)[:, q0:TB], ks[p][:, h, kt * P:(kt + 1) * P],
                                          qs[p][:, h, j * TB + q0:(j + 1) * TB], start=True, stop=not DIAG[u])
                    if DIAG[u]:
                        mm = nc.tensor.matmul(bank(n % SB)[:, q0:q0 + P], causal_b[:, :], ident_b[:, :],
                                              start=False, stop=True)
                    mm.then_inc(s_mm[p], 1)

                def p_v(p, i, u):
                    j, kt, q0 = UNITS[u]
                    if u == 0:
                        pe.wait_ge(v_in[p], FIRST + 16 * (i + 1))
                        pe.wait_ge(ctx_done[1 - p], FIRST + BPB * (i + p))
                    elif kt == 0:
                        pe.wait_ge(ctx_done[p], FIRST + BPB * i + j)
                    pe.wait_ge(exp_done[p], FIRST + NS * i + HG * (u + 1))
                    for h in range(HG):
                        mm = nc.tensor.matmul(bank(3)[VW * h:VW * (h + 1), q0:TB], vs[p][:, kt, h, :],
                                              probs[u % PB][:, h, q0:TB], start=(kt == 0),
                                              stop=(kt == TT * (j + 1) - 1))
                    mm.then_inc(pv_mm[p], 1)

                def step(p, i, before=True, more=True):
                    def chunks(n):
                        if more:
                            for c in PLAN[n]:
                                max_chunk(*following(p, i), c)

                    for u in range(NU):
                        score(p, i, u, 0)
                        chunks(POINTS * u)
                        score(p, i, u, 1)
                        chunks(POINTS * u + 1)
                        if u >= LAG:
                            p_v(p, i, u - LAG)
                        elif before:
                            p_v(*preceding(p, i), NU - LAG + u)
                        chunks(POINTS * u + 2)
                        score(p, i, u, 2)
                        chunks(POINTS * u + 3)
                        score(p, i, u, 3)
                        chunks(POINTS * u + 4)
                        if more and u == PLAN_LAST + 1:
                            max_turn(*following(p, i))

                for c in range(NC):
                    max_chunk(0, 0, c)
                max_turn(0, 0)
                step(0, 0, before=False)
                with pe.Fori(0, last) as i:
                    step(1, i)
                    step(0, i + 1)
                step(1, last, more=False)
                for u in range(NU - LAG, NU):
                    p_v(1, last, u)


def block3(nc, sb_, sem, sems, counts, bank, x, contexts, w1, w2, wo_s, rw_s, ident, mod_t, gates, w_in, out):
    with ExitStack() as own:
        def sb(name, shape, dt=F32):
            return sb_(name, shape, dt, own)

        num = [sb(f"num{p}", [P, KK, TB]) for p in range(2)]
        den = [sb(f"den{p}", [P, KK, TB]) for p in range(2)]
        xres = [sb(f"xres{p}", [P, TT, D]) for p in range(2)]
        gated = sb("gated", [P, TT, D])
        stats = sb("stats_b", [P, TT, 6])
        mv = sb("mv_b", [P, TT, 2])
        rstd = sb("rstd_b", [P, TT])
        xn = sb("xn_b", [P, TT, D])
        h2t = sb("h2t", [P, KK, TB])
        h2_hi = [sb(f"h2_hi{p}", [P, KK, TB], F32R) for p in range(2)]
        h2_lo = [sb(f"h2_lo{p}", [P, KK, TB], F32R) for p in range(2)]
        w1_hi, w1_lo = (sb(f"w1_{n}", [P, KK, NW * P], F32R) for n in ("hi", "lo"))
        w2_hi, w2_lo = (sb(f"w2_{n}", [P, NW, D], F32R) for n in ("hi", "lo"))
        stage = [sb(f"stage{k}", [P, NW * P // 2]) for k in range(2)]
        gate_e = sb("gate_e", [P, TT, E])
        prob = sb("prob", [P, TT, E])
        rank = sb("rank", [P, TT, E])
        beats = sb("beats", [P, TT, E])
        top = sb("top", [P, TT, E])
        top_sum = sb("top_sum", [P, TT])
        combine = [sb(f"combine{p}", [P, TT, E]) for p in range(2)]
        relu = [sb(f"relu{k}", [P, TB]) for k in range(2)]
        hid = [sb(f"hid{k}", [P, TB]) for k in range(2)]
        hid_hi = [sb(f"hid_hi{k}", [P, TB], F32R) for k in range(HB)]
        hid_lo = [sb(f"hid_lo{k}", [P, TB], F32R) for k in range(HB)]
        mix = [sb(f"mix{p}", [P, TT, D]) for p in range(2)]
        res = [sb(f"res{p}", [P, TT, D]) for p in range(2)]

        ctx_in, x_in = sems("ctx_in"), sems("xres_in")
        den_inv, ctx_norm = sems("den_inv"), sems("ctx_norm")
        rooted, inverted = sems("rooted_b"), sems("inverted_b")
        o_mm, res_done, ln_steps = sems("o_mm"), sems("res_done"), sems("ln_steps")
        t_mm, h_done = sems("t2_mm"), sems("h2_done")
        r_mm, r_exp, r_steps = sems("r_mm"), sems("r_exp"), sems("r_steps")
        hi_done, lo_done = sems("hi_done"), sems("lo_done")
        h_hi, h_lo = sems("h_hi"), sems("h_lo")
        w_hi, w_lo = sem("w_hi"), sem("w_lo")
        stage_in = [sem(f"stage_in{k}") for k in range(2)]
        pool_lo = sems("pool_lo")
        u_mm, relu_done, hid_done, d_mm = sems("u_mm"), sems("relu_done"), sems("hid_done"), sems("d_mm")
        mix_done, final, out_done = sems("mix_done"), sems("final"), sems("out_done")
        last = NBLK // 2 - 1
        pieces = []
        for k in range(KK):
            for half in range(2):
                cols = slice(half * NW * P // 2, (half + 1) * NW * P // 2)
                pieces.append((w1[k * P:(k + 1) * P, cols], w1_hi[:, k, cols], w1_lo[:, k, cols]))
        for k in range(4):
            tiles = slice(k * NW // 4, (k + 1) * NW // 4)
            pieces.append((w2[k * NW // 4 * P:(k + 1) * NW // 4 * P, :].rearrange("(t p) n -> p t n", p=P),
                           w2_hi[:, tiles, :], w2_lo[:, tiles, :]))

        def staged(q):
            s = stage[q % 2][:, :]
            return s if q < 4 else s.rearrange("p (t n) -> p t n", n=D)

        RS = 3 + 2 * E + 5

        def batch(p, i):
            return (2 * i + p) // BPB if isinstance(i, int) else i // (BPB // 2)

        sp_passed, dve_passed = sem("sp_passed_b"), sem("dve_passed_b")
        count_from_first(nc, counts)
        def low_part(engine, ops, p, i, w):
            engine.wait_ge(hi_done[p], FIRST + NW * i + w + 1)
            which = lo_done[p] if w not in POOL_LO else pool_lo[p]
            ops.tensor_tensor(hid_lo[w % HB][:, :], hid[w % 2][:, :], hid_hi[w % HB][:, :].bitcast(F32),
                              ALU.subtract).then_inc(which, 1)

        def low_parts_done(engine, p, i, w):
            on_pool = sum(v in POOL_LO for v in range(w + 1))
            engine.wait_ge(lo_done[p], FIRST + (NW - len(POOL_LO)) * i + w + 1 - on_pool)
            engine.wait_ge(pool_lo[p], FIRST + len(POOL_LO) * i + on_pool)

        with nc.Block() as block:
            @block.sync
            def _(sp):
                sp.wait_ge(w_in, 32)

                def load_contexts(p, i):
                    n = 2 * i + p
                    wait_apart(sp, o_mm[p], FIRST + TT * i, sp_passed)
                    cols = bass.ds(n * TB, TB)
                    for k in range(KK):
                        rows = contexts[k * H // KK * VW:(k + 1) * H // KK * VW, cols].rearrange(
                            "(h c) t -> h c t", c=VW)
                        sp.dma_start(num[p][:, k, :], rows[:, 0:DK, :]).then_inc(ctx_in[p], 16)
                        sp.dma_start(den[p][:, k, :], rows[:, DK:VW, :]).then_inc(ctx_in[p], 16)

                def load_x(p, i):
                    cols = bass.ds((2 * i + p) * TB, TB)
                    wait_apart(sp, final[p], FIRST + 2 * TT * i, sp_passed)
                    sp.dma_start(xres[p][:, :, :], x[cols, :].rearrange("(t p) d -> p t d", p=P)
                                 ).then_inc(x_in[p], 16)

                def store(p, i):
                    wait_apart(sp, final[p], FIRST + 2 * TT * (i + 1), sp_passed)
                    sp.dma_start(out[bass.ds((2 * i + p) * TB, TB), :].rearrange("(t p) d -> p t d", p=P),
                                 res[p][:, :, :]).then_inc(out_done[p], 16)

                def load_piece(q):
                    if q >= 2:
                        sp.wait_ge(w_lo, q - 1)
                    sp.dma_start(staged(q), pieces[q][0]).then_inc(stage_in[q % 2], 16)

                load_contexts(0, 0)
                load_piece(0)
                load_x(0, 0)
                load_piece(1)
                load_piece(2)
                load_piece(3)
                load_contexts(1, 0)
                load_x(1, 0)
                for q in range(4, 8):
                    load_piece(q)
                with sp.Fori(0, last) as i:
                    for p in range(2):
                        load_contexts(p, i + 1)
                        store(p, i)
                        load_x(p, i + 1)
                for p in range(2):
                    store(p, last)
                for p in range(2):
                    sp.wait_ge(out_done[p], FIRST + 16 * (last + 1))

            @block.gpsimd
            def _(pool):
                for q, (_, hi, lo) in enumerate(pieces):
                    pool.wait_ge(w_hi, q + 1)
                    nc.gpsimd.tensor_tensor(lo, staged(q), hi.bitcast(F32), ALU.subtract).then_inc(w_lo, 1)

                def step(p, i, b):
                    for w in POOL_LO:
                        low_part(pool, nc.gpsimd, p, i, w)
                    pool.wait_ge(out_done[p], FIRST + 16 * i)
                    pool.wait_ge(mix_done[p], FIRST + TT * E * (i + 1))
                    for t in range(TT):
                        nc.gpsimd.tensor_tensor(res[p][:, t, :], mix[p][:, t, :],
                                                gates[:, bass.ds(b, 1), D:2 * D].squeeze(1), ALU.mult
                                                ).then_inc(final[p], 1)
                    for t in range(TT):
                        pool.wait_ge(final[p], FIRST + 2 * TT * i + t + 1)
                        nc.gpsimd.tensor_tensor(res[p][:, t, :], res[p][:, t, :], xres[p][:, t, :], ALU.add
                                                ).then_inc(final[p], 1)

                with pool.Fori(0, last + 1) as i:
                    for p in range(2):
                        step(p, i, batch(p, i))

            @block.scalar
            def _(act):
                def router_exp(p, i):
                    act.wait_ge(r_mm[p], FIRST + i + 1)
                    act.wait_ge(r_steps[1 - p], FIRST + RS * (i + p))
                    nc.scalar.activation(gate_e[:, :, :], bank(6)[:, 0:TT * E].rearrange("p (t e) -> p t e", e=E),
                                         ACT.Exp, scale=-1.0).then_inc(r_exp[p], 1)

                def root(p, i):
                    act.wait_ge(ln_steps[p], FIRST + (4 * TT + 1) * (i + 1))
                    nc.scalar.activation(rstd[:, :], rstd[:, :], ACT.Sqrt).then_inc(rooted[p], 1)

                def high_h2(p, i):
                    act.wait_ge(h_done[p], FIRST + KK * (i + 1))
                    act.wait_ge(u_mm[p], FIRST + NW * i)
                    nc.scalar.activation(h2_hi[p][:, :, :], h2t[:, :, :], ACT.Copy).then_inc(h_hi[p], 1)

                def step(p, i, more=True):
                    for w in range(NW + 1):
                        if w < NW:
                            act.wait_ge(u_mm[p], FIRST + NW * i + w + 1)
                            if w >= 2:
                                act.wait_ge(hid_done[p], FIRST + NW * i + w - 1)
                            elif w == 0:
                                act.wait_ge(hid_done[1 - p], FIRST + NW * (i + p))
                            nc.scalar.activation(relu[w % 2][:, :], bank(w % 2), ACT.Relu).then_inc(relu_done[p], 1)
                        if w >= 1:
                            v = w - 1
                            act.wait_ge(hid_done[p], FIRST + NW * i + v + 1)
                            if v >= HB:
                                act.wait_ge(d_mm[p], FIRST + NW * i + v - HB + 1)
                            elif v == 0:
                                act.wait_ge(d_mm[1 - p], FIRST + NW * (i + p))
                            nc.scalar.activation(hid_hi[v % HB][:, :], hid[v % 2][:, :], ACT.Copy
                                                 ).then_inc(hi_done[p], 1)
                        if w == 8 and more:
                            root(*following(p, i))
                        if w == 13 and more:
                            high_h2(*following(p, i))
                        if w == 16 and more:
                            router_exp(*following(p, i))

                for q, (_, hi, _) in enumerate(pieces[:4]):
                    act.wait_ge(stage_in[q % 2], 16 * (q // 2 + 1))
                    nc.scalar.activation(hi, staged(q), ACT.Copy).then_inc(w_hi, 1)
                root(0, 0)
                high_h2(0, 0)
                router_exp(0, 0)
                for q, (_, hi, _) in list(enumerate(pieces))[4:]:
                    act.wait_ge(stage_in[q % 2], 16 * (q // 2 + 1))
                    nc.scalar.activation(hi, staged(q), ACT.Copy).then_inc(w_hi, 1)
                with act.Fori(0, last) as i:
                    for p in range(2):
                        step(p, i)
                step(0, last)
                step(1, last, more=False)

            @block.vector
            def _(dve):
                def inverse_denominators(p, i, quarter):
                    if quarter == 0:
                        dve.wait_ge(ctx_in[p], FIRST + 64 * (i + 1))
                    k, half = quarter // 2, slice(quarter % 2 * TB // 2, (quarter % 2 + 1) * TB // 2)
                    nc.vector.reciprocal(den[p][:, k, half], den[p][:, k, half]).then_inc(den_inv[p], 1)

                def contexts_over_denominators(p, i):
                    dve.wait_ge(den_inv[p], FIRST + 4 * (i + 1))
                    nc.vector.tensor_tensor(num[p][:, :, :], num[p][:, :, :], den[p][:, :, :], ALU.mult
                                            ).then_inc(ctx_norm[p], 1)

                def residual(p, i, b):
                    dve.wait_ge(x_in[p], FIRST + 16 * (i + 1))
                    dve.wait_ge(t_mm[1 - p], FIRST + KK * (i + p))
                    n = 4 * TT + 1
                    for t in range(TT):
                        dve.wait_ge(o_mm[p], FIRST + TT * i + 2 * (t // 2) + 2)
                        nc.vector.tensor_tensor(gated[:, t, :], bank(6 + t // 2)[:, (t % 2) * D:(t % 2 + 1) * D],
                                                gates[:, bass.ds(b, 1), 0:D].squeeze(1), ALU.mult
                                                ).then_inc(ln_steps[p], 1)
                    for t in range(TT):
                        dve.wait_ge(ln_steps[p], FIRST + n * i + t + 1)
                        nc.vector.tensor_tensor(xres[p][:, t, :], gated[:, t, :], xres[p][:, t, :], ALU.add
                                                ).then_inc(ln_steps[p], 1)
                    for t in range(TT):
                        dve.wait_ge(ln_steps[p], FIRST + n * i + TT + t + 1)
                        nc.vector.bn_stats(stats[:, t, :], xres[p][:, t, :]).then_inc(ln_steps[p], 1)
                    for t in range(TT):
                        wait_apart(dve, ln_steps[p], FIRST + n * i + 2 * TT + t + 1, dve_passed)
                        nc.vector.bn_aggr(mv[:, t, :], stats[:, t, :]).then_inc(ln_steps[p], 1)
                    dve.wait_ge(ln_steps[p], FIRST + n * i + 4 * TT)
                    nc.vector.tensor_scalar(rstd[:, :], mv[:, :, 1], EPS, None, ALU.add
                                            ).then_inc(ln_steps[p], 1)

                def normalise(p, i):
                    dve.wait_ge(rooted[p], FIRST + i + 1)
                    nc.vector.reciprocal(rstd[:, :], rstd[:, :]).then_inc(inverted[p], 1)
                    dve.wait_ge(inverted[p], FIRST + i + 1)
                    for t in range(TT):
                        nc.vector.tensor_scalar(xn[:, t, :], xres[p][:, t, :], mv[:, t, 0:1], rstd[:, t:t + 1],
                                                ALU.subtract, ALU.mult).then_inc(res_done[p], 1)

                def modulate(p, i, b):
                    dve.wait_ge(r_mm[1 - p], FIRST + i + p)
                    dve.wait_ge(h_hi[1 - p], FIRST + i + p)
                    for k in range(KK):
                        dve.wait_ge(t_mm[p], FIRST + KK * i + k + 1)
                        nc.vector.tensor_scalar(h2t[:, k, :], bank(6 + k), mod_t[:, 3, k, bass.ds(b, 1)],
                                                mod_t[:, 2, k, bass.ds(b, 1)], ALU.mult, ALU.add
                                                ).then_inc(h_done[p], 1)

                def low_h2(p, i):
                    dve.wait_ge(h_hi[p], FIRST + i + 1)
                    nc.vector.tensor_tensor(h2_lo[p][:, :, :], h2t[:, :, :], h2_hi[p][:, :, :].bitcast(F32),
                                            ALU.subtract).then_inc(h_lo[p], 1)

                def router(p, i):
                    n = [RS * i]

                    def linked(ins):
                        ins.then_inc(r_steps[p], 1)
                        n[0] = n[0] + 1
                        dve.wait_ge(r_steps[p], FIRST + n[0])

                    dve.wait_ge(r_exp[p], FIRST + i + 1)
                    dve.wait_ge(mix_done[p], FIRST + TT * E * i)
                    linked(nc.vector.tensor_scalar(gate_e[:, :, :], gate_e[:, :, :], 1.0, None, ALU.add))
                    linked(nc.vector.reciprocal(prob[:, :, :], gate_e[:, :, :]))
                    linked(nc.vector.memset(rank[:, :, :], 0.0))
                    for e in range(E):
                        one = prob[:, :, e:e + 1]
                        nc.vector.tensor_tensor(beats[:, :, 0:e + 1], one.to_broadcast([P, TT, e + 1]),
                                                prob[:, :, 0:e + 1], ALU.is_gt)
                        if e + 1 < E:
                            nc.vector.tensor_tensor(beats[:, :, e + 1:E], one.to_broadcast([P, TT, E - e - 1]),
                                                    prob[:, :, e + 1:E], ALU.is_ge).then_inc(r_steps[p], 1)
                        else:
                            nc.vector.engine_nop().then_inc(r_steps[p], 1)
                        n[0] = n[0] + 1
                        dve.wait_ge(r_steps[p], FIRST + n[0])
                        linked(nc.vector.tensor_tensor(rank[:, :, :], rank[:, :, :], beats[:, :, :], ALU.add))
                    linked(nc.vector.scalar_tensor_tensor(out=top[:, :, :], in0=rank[:, :, :], scalar=2.0,
                                                          in1=prob[:, :, :], op0=ALU.is_lt, op1=ALU.mult))
                    linked(nc.vector.tensor_reduce(top_sum[:, :], top[:, :, :], AX.X, ALU.add))
                    linked(nc.vector.tensor_scalar(top_sum[:, :], top_sum[:, :], 1e-20, None, ALU.add))
                    linked(nc.vector.reciprocal(top_sum[:, :], top_sum[:, :]))
                    linked(nc.vector.tensor_tensor(combine[p][:, :, :], top[:, :, :],
                                                   top_sum[:, :].unsqueeze(2).to_broadcast([P, TT, E]), ALU.mult))

                def hidden(p, i, w):
                    dve.wait_ge(relu_done[p], FIRST + NW * i + w + 1)
                    if w >= 2:
                        low_parts_done(dve, p, i, w - 2)
                    elif w == 0:
                        low_parts_done(dve, 1 - p, i + p - 1, NW - 1)
                    nc.vector.tensor_tensor(hid[w % 2][:, :], bank(w % 2), relu[w % 2][:, :], ALU.mult
                                            ).then_inc(hid_done[p], 1)

                def mixed(p, i, e):
                    dve.wait_ge(d_mm[p], FIRST + NW * i + FIRST_W[e] + FT[e])
                    if e == 0:
                        dve.wait_ge(final[p], FIRST + 2 * TT * i)
                    for t in range(TT):
                        y = bank(2 + 2 * (e % 2) + t // 2)[:, (t % 2) * D:(t % 2 + 1) * D]
                        share = combine[p][:, t, e:e + 1]
                        if e == 0:
                            nc.vector.tensor_scalar(mix[p][:, t, :], y, share, None, ALU.mult
                                                    ).then_inc(mix_done[p], 1)
                        else:
                            dve.wait_ge(mix_done[p], FIRST + TT * E * i + TT * (e - 1) + t + 1)
                            nc.vector.scalar_tensor_tensor(out=mix[p][:, t, :], in0=y, scalar=share,
                                                           in1=mix[p][:, t, :], op0=ALU.mult, op1=ALU.add
                                                           ).then_inc(mix_done[p], 1)

                def step(p, i, more=True):
                    nxt = following(p, i)
                    b = batch(*nxt)
                    for w in range(NW + 1):
                        if w < NW:
                            hidden(p, i, w)
                        if w >= 1 and w - 1 not in POOL_LO:
                            low_part(dve, nc.vector, p, i, w - 1)
                        if more and w < 4:
                            inverse_denominators(*nxt, w)
                        if more and w == 4:
                            contexts_over_denominators(*nxt)
                        if more and w == 7:
                            residual(*nxt, b)
                        if more and w == 9:
                            normalise(*nxt)
                        if more and w == 13:
                            modulate(*nxt, b)
                        if more and w == 15:
                            low_h2(*nxt)
                        if more and w == 18:
                            router(*nxt)
                        if 3 <= w < NW and EXPERT[w - 3] != EXPERT[w - 2]:
                            mixed(p, i, EXPERT[w - 3])
                        if w == NW and EXPERT[w - 3] != EXPERT[w - 2]:
                            mixed(p, i, EXPERT[w - 3])
                    mixed(p, i, E - 1)

                for quarter in range(4):
                    inverse_denominators(0, 0, quarter)
                contexts_over_denominators(0, 0)
                residual(0, 0, 0)
                normalise(0, 0)
                modulate(0, 0, 0)
                low_h2(0, 0)
                router(0, 0)
                with dve.Fori(0, last) as i:
                    for p in range(2):
                        step(p, i)
                step(0, last)
                step(1, last, more=False)

            @block.tensor
            def _(pe):
                pe.wait_ge(w_in, 32)

                def project(p, i):
                    pe.wait_ge(ctx_norm[p], FIRST + i + 1)
                    pe.wait_ge(r_exp[1 - p], FIRST + i + p)
                    for t in range(TT):
                        o = bank(6 + t // 2)[:, (t % 2) * D:(t % 2 + 1) * D]
                        for k in range(KK):
                            mm = nc.tensor.matmul(o, num[p][:, k, t * P:(t + 1) * P], wo_s[:, k, :],
                                                  start=(k == 0), stop=(k == KK - 1))
                        mm.then_inc(o_mm[p], 1)

                def transposes(p, i):
                    pe.wait_ge(res_done[p], FIRST + TT * (i + 1))
                    for k in range(KK):
                        for t in range(TT):
                            mm = nc.tensor.transpose(bank(6 + k)[:, t * P:(t + 1) * P],
                                                     xn[:, t, k * P:(k + 1) * P], ident[:, :])
                        mm.then_inc(t_mm[p], 1)

                def route(p, i):
                    pe.wait_ge(h_done[p], FIRST + KK * (i + 1))
                    for t in range(TT):
                        for k in range(KK):
                            mm = nc.tensor.matmul(bank(6)[:, t * E:(t + 1) * E], h2t[:, k, t * P:(t + 1) * P],
                                                  rw_s[:, k, :], start=(k == 0), stop=(k == KK - 1))
                    mm.then_inc(r_mm[p], 1)

                def up(p, i, w):
                    if w == 0:
                        pe.wait_ge(h_lo[p], FIRST + i + 1)
                        pe.wait_ge(hid_done[1 - p], FIRST + NW * (i + p))
                    elif w >= 2:
                        pe.wait_ge(hid_done[p], FIRST + NW * i + w - 1)
                    cols = slice(w * P, (w + 1) * P)
                    for k in range(KK):
                        nc.tensor.matmul(bank(w % 2), w1_hi[:, k, cols], h2_hi[p][:, k, :],
                                         start=(k == 0), stop=False)
                        nc.tensor.matmul(bank(w % 2), w1_hi[:, k, cols], h2_lo[p][:, k, :], start=False, stop=False)
                        mm = nc.tensor.matmul(bank(w % 2), w1_lo[:, k, cols], h2_hi[p][:, k, :],
                                              start=False, stop=(k == KK - 1))
                    mm.then_inc(u_mm[p], 1)

                def down(p, i, w):
                    e = EXPERT[w]
                    low_parts_done(pe, p, i, w)
                    if w == FIRST_W[e]:
                        if e >= 2:
                            pe.wait_ge(mix_done[p], FIRST + TT * (E * i + e - 1))
                        else:
                            pe.wait_ge(mix_done[1 - p], FIRST + TT * E * (i + p))
                    for t in range(TT):
                        y = bank(2 + 2 * (e % 2) + t // 2)[:, (t % 2) * D:(t % 2 + 1) * D]
                        hi, lo = (h[w % HB][:, t * P:(t + 1) * P] for h in (hid_hi, hid_lo))
                        nc.tensor.matmul(y, hi, w2_hi[:, w, :], start=(w == FIRST_W[e] and t % 2 == 0),
                                         stop=False, skip_group_check=True)
                        nc.tensor.matmul(y, hi, w2_lo[:, w, :], start=False, stop=False, skip_group_check=True)
                        mm = nc.tensor.matmul(y, lo, w2_hi[:, w, :], start=False,
                                              stop=(w == FIRST_W[e] + FT[e] - 1), skip_group_check=True)
                    mm.then_inc(d_mm[p], 1)

                def step(p, i, more=True):
                    nxt = following(p, i)
                    up(p, i, 0)
                    up(p, i, 1)
                    for w in range(NW):
                        if w + 2 < NW:
                            up(p, i, w + 2)
                        down(p, i, w)
                        if more and w == 5:
                            project(*nxt)
                        if more and w == 11:
                            transposes(*nxt)
                        if more and w == 14:
                            route(*nxt)

                project(0, 0)
                transposes(0, 0)
                route(0, 0)
                pe.wait_ge(w_lo, len(pieces))
                with pe.Fori(0, last) as i:
                    for p in range(2):
                        step(p, i)
                step(0, last)
                step(1, last, more=False)


def kernel(L0_attn_x, L0_attn_W_qkv, L0_attn_W_o, L0_ffn_router_w, L0_ffn_w1, L0_ffn_w2, L0_c, L0_wmod):
    import numpy as np
    import concourse.bacc as bacc
    from concourse.bass_utils import run_bass_kernel_spmd

    laid = {
        "x": np.asarray(L0_attn_x).reshape(T, D),
        "wqkv_t": np.asarray(L0_attn_W_qkv).reshape(3 * D, D).T,
        "wo_t": np.asarray(L0_attn_W_o).T,
        "rw_t": np.asarray(L0_ffn_router_w).T,
        "w1": np.asarray(L0_ffn_w1),
        "w2": np.asarray(L0_ffn_w2),
        "c_t": np.asarray(L0_c).T,
        "wmod": np.asarray(L0_wmod),
    }
    nc = bacc.Bacc("TRN2", target_bir_lowering=False, num_devices=1)
    nc.disable_value_cache = True
    arrays, args = {}, []
    for name, a in laid.items():
        arrays[f"in_{name}"] = np.ascontiguousarray(a)
        args.append(nc.dram_tensor(f"in_{name}", a.shape, F32, kind="ExternalInput").ap())
    args.append(nc.dram_tensor("out_0", (T, D), F32, kind="ExternalOutput").ap())
    adaln_layer(nc, *args)
    r = run_bass_kernel_spmd(nc, [arrays], core_ids=[0])
    return r.results[0]["out_0"].reshape(B, S, D)
```

```python
from contextlib import ExitStack

import concourse.bass as bass
from concourse import mybir

F32 = mybir.dt.float32
F32R = mybir.dt.float32r
BF16 = mybir.dt.bfloat16
ALU = mybir.AluOpType
ACT = mybir.ActivationFunctionType
AX = mybir.AxisListType

P = 128
B, S, D, H = 4, 2048, 256, 16
DK = D // H
T = B * S
KK = D // P
TB = 512
TT = TB // P
NBLK = T // TB
BPB = S // TB
SCALE = DK ** -0.5
EPS = 1e-5
NEG = -1e30

HG = 4
NG = B * H // HG
QT = S // P
PARTS = 3
STACK = 6 * DK
VW = 2 * DK

WIDTHS = [256] * 4 + [512] * 4
E = len(WIDTHS)
FT = [w // P for w in WIDTHS]
NW = sum(FT)
EXPERT = [e for e in range(E) for _ in range(FT[e])]
FIRST_W = [sum(FT[:e]) for e in range(E)]

UNITS = [(j, kt, max(0, kt - TT * j) * P) for j in range(BPB) for kt in range(TT * (j + 1))]
NU = len(UNITS)
NS = HG * NU
DIAG = [kt >= TT * j for j, kt, _ in UNITS]
UNITS_TO = [TT * (j + 1) * (j + 2) // 2 for j in range(BPB)]
FIRST = 1
LAG = 2
POOL_LO = [w for w in range(NW) if w % 3 == 2]
QK_BEFORE = 1
HIGH_AFTER = 2
HB = 4
MIX_LAG = 4
OUT_AT = 1
RANKS = {20: range(0, 2), 21: range(2, 4), 22: range(4, 6), 24: range(6, E)}
INVERSE = (1, 2, 4, 6)
CONTEXTS, PROJECT = 8, 8
GATE, RESIDUAL, STATISTICS, NORMALISE, TRANSPOSE = 10, 12, 13, 14, 15
MODULATE, LOW, ROUTE, SHARES = 17, 18, 18, 24
HF = 4
SB = 3
PB = 4

CW = 512
MS = 4
CHUNKS = [
    (h, t, k0, min(CW, P * (t + 1) - k0), k0 + CW >= P * (t + 1))
    for h in range(HG) for t in range(QT) for k0 in range(0, P * (t + 1), CW)
]
NC = len(CHUNKS)


def chunk_plan():
    steps = [(n, k) for n in range(PLAN_FIRST, PLAN_LAST) for k in range(POINTS)]
    main_cost = [TB - q0 + STEP_COST for _, _, q0 in UNITS]
    chunk_cost = [w + STEP_COST for *_, w, _ in CHUNKS]
    span, total = sum(main_cost[n] for n, _ in steps), sum(chunk_cost)
    plan, c, done, spent = [[] for _ in range(POINTS * NU)], 0, 0, 0
    for n, k in steps:
        spent += main_cost[n]
        while c < NC and done * span < spent * total:
            plan[POINTS * n + k].append(c)
            done += chunk_cost[c]
            c += 1
    return plan


STEP_COST = 64
POINTS = 5
PLAN_FIRST, PLAN_LAST = 3, NU - 4
PLAN = chunk_plan()


def count_from_first(nc, counts):
    with nc.Block() as block:
        @block.sync
        def _(sp):
            for s in counts[0::4]:
                sp.sem_inc(s, FIRST)

        @block.scalar
        def _(act):
            for s in counts[1::4]:
                act.sem_inc(s, FIRST)

        @block.vector
        def _(dve):
            for s in counts[2::4]:
                dve.sem_inc(s, FIRST)

        @block.gpsimd
        def _(pool):
            for s in counts[3::4]:
                pool.sem_inc(s, FIRST)

    counts.clear()


def wait_apart(engine, semaphore, value, passed):
    engine.wait_ge(semaphore, value)
    engine.sem_inc(passed, 1)


def following(p, i):
    return 1 - p, i + p


def adaln_layer(nc, x, wqkv_t, wo_t, rw_t, w1, w2, c_t, wmod, out):
    q_parts = nc.dram_tensor("q_parts", (D, PARTS, T), BF16, kind="Internal").ap()
    k_parts = nc.dram_tensor("k_parts", (D, PARTS, T), BF16, kind="Internal").ap()
    v_ones = nc.dram_tensor("v_ones", (T, H * VW), F32, kind="Internal").ap()
    contexts = nc.dram_tensor("contexts", (H * VW, T), F32, kind="Internal").ap()

    with ExitStack() as whole:
        def sb(name, shape, dt=F32, at=whole):
            return at.enter_context(nc.sbuf_tensor(name, shape, dt))

        def sem(name):
            return whole.enter_context(nc.semaphore(name))

        counts = []

        def sems(name, n=2):
            made = [sem(f"{name}{k}") for k in range(n)]
            counts.extend(made)
            return made

        ps = whole.enter_context(nc.psum_tensor("ps", [P, 8 * 512], F32))

        def bank(n, count=1):
            return ps[:, n * 512:(n + count) * 512]

        wo_s = sb("wo_s", [P, KK, D])
        rw_s = sb("rw_s", [P, KK, E])
        ident = sb("ident", [P, P])
        mod_t = sb("mod_t", [P, 4, KK, B])
        gates = sb("gates", [P, B, 2 * D])

        w_in = sem("w_in")
        block1(nc, sb, sem, sems, counts, bank, x, wqkv_t, wo_t, rw_t, c_t, wmod, q_parts, k_parts, v_ones,
               wo_s, rw_s, ident, mod_t, gates, w_in)
        block2(nc, sb, sem, sems, counts, bank, q_parts, k_parts, v_ones, contexts, ident)
        block3(nc, sb, sem, sems, counts, bank, x, contexts, w1, w2, wo_s, rw_s, ident, mod_t, gates, w_in, out)


def preceding(p, i):
    return 1 - p, i + p - 1


def block1(nc, sb_, sem, sems, counts, bank, x, wqkv_t, wo_t, rw_t, c_t, wmod, q_parts, k_parts, v_ones,
           wo_s, rw_s, ident, mod_t, gates, w_in):
    with ExitStack() as own:
        def sb(name, shape, dt=F32):
            return sb_(name, shape, dt, own)

        wqkv_s = sb("wqkv_s", [P, KK, 3 * D])
        wmod_s = sb("wmod_s", [P, KK, 6 * D])
        ct = sb("ct", [P, KK, B])
        ce = sb("ce", [P, KK, B])
        silu = sb("silu", [P, KK, B])
        silu_all = sb("silu_all", [P, KK, B, P])
        sign = sb("sign", [P, B, 2 * D])
        size = sb("size", [P, B, 2 * D])
        xin = [sb(f"xin{p}", [P, TT, D]) for p in range(2)]
        stats = [sb(f"stats{p}", [P, TT, 6]) for p in range(2)]
        mv = [sb(f"mv{p}", [P, TT, 2]) for p in range(2)]
        rstd = [sb(f"rstd{p}", [P, TT]) for p in range(2)]
        xn = [sb(f"xn{p}", [P, TT, D]) for p in range(2)]
        ht = [sb(f"ht{p}", [P, KK, TB]) for p in range(2)]
        ht_hi = [sb(f"ht_hi{p}", [P, KK, TB], F32R) for p in range(2)]
        ht_lo = [sb(f"ht_lo{p}", [P, KK, TB], F32R) for p in range(2)]
        wqkv_hi, wqkv_lo = (sb(f"wqkv_{n}", [P, KK, 3 * D], F32R) for n in ("hi", "lo"))
        rest = sb("rest", [P, 4, TB])
        parts = [sb(f"parts{p}", [P, 4, PARTS, TB], BF16) for p in range(2)]
        vt = [sb(f"vt{p}", [P, TT, H, VW]) for p in range(2)]

        setup_in = sem("setup_in")
        id_zero, id_done = sem("id_zero"), sem("id_done")
        c_steps, c_exp = sem("c_steps"), sem("c_exp")
        mod_mm, gate_mm = sem("mod_mm"), sem("gate_mm")
        gate_steps = sem("gate_steps")
        ones_set = sem("ones_set")
        wqkv_split = sem("wqkv_split")
        ht_high, ht_low = sems("ht_high"), sems("ht_low")
        x_in, stat_done, xn_done = sems("x_in"), sems("stat_done"), sems("xn_done")
        rooted, inverted = sems("rooted"), sems("inverted")
        t_mm, ht_done = sems("t_mm"), sems("ht_done")
        qk_mm, part1, rest1, part2, part3 = (sems(n) for n in ("qk_mm", "part1_", "rest1_", "part2_", "part3_"))
        v_mm, v_done = sems("v_mm"), sems("v_done")
        stored = sems("stored")

        sp_passed, dve_passed = sem("sp_passed"), sem("dve_passed")
        count_from_first(nc, counts)
        with nc.Block() as block:
            @block.sync
            def _(sp):
                sp.dma_start(ct[:, :, :], c_t.rearrange("(k p) b -> p k b", p=P)).then_inc(setup_in, 16)
                sp.dma_start(wmod_s[:, :, :], wmod.rearrange("(k p) n -> p k n", p=P)).then_inc(setup_in, 16)
                sp.dma_start(wqkv_s[:, :, :], wqkv_t.rearrange("(k p) n -> p k n", p=P)).then_inc(setup_in, 16)

                def store(p, i):
                    cols = bass.ds((2 * i + p) * TB, TB)
                    for o in range(4):
                        to = (q_parts, k_parts)[o // 2]
                        wait_apart(sp, part3[p], FIRST + 4 * i + o + 1, sp_passed)
                        sp.dma_start(to[P * (o % 2):P * (o % 2 + 1), :, cols],
                                     parts[p][:, o, :, :]).then_inc(stored[p], 16)
                    wait_apart(sp, v_done[p], FIRST + 2 * (i + 1), sp_passed)
                    sp.dma_start(v_ones[cols, :].rearrange("(t p) c -> p t c", p=P),
                                 vt[p][:, :, :, :].rearrange("p t h c -> p t (h c)")).then_inc(stored[p], 16)

                sp.dma_start(wo_s[:, :, :], wo_t.rearrange("(k p) n -> p k n", p=P)).then_inc(w_in, 16)
                sp.dma_start(rw_s[:, :, :], rw_t.rearrange("(k p) n -> p k n", p=P)).then_inc(w_in, 16)
                with sp.Fori(0, NBLK // 2) as i:
                    for p in range(2):
                        store(p, i)
                for p in range(2):
                    sp.wait_ge(stored[p], FIRST + 16 * 5 * NBLK // 2)

            @block.gpsimd
            def _(pool):
                nc.gpsimd.memset(ident[:, :], 0.0).then_inc(id_zero, 1)
                pool.wait_ge(id_zero, 1)
                nc.gpsimd.affine_select(out=ident[:, :], in_=ident[:, :], compare_op=ALU.not_equal, fill=1.0,
                                        base=0, pattern=[[-1, P]], channel_multiplier=1).then_inc(id_done, 1)
                for p in range(2):
                    nc.gpsimd.memset(vt[p][:, :, :, DK:VW], 1.0).then_inc(ones_set, 1)
                pool.wait_ge(wqkv_split, 1)
                nc.gpsimd.tensor_tensor(wqkv_lo[:, :, :], wqkv_s[:, :, :], wqkv_hi[:, :, :].bitcast(F32),
                                        ALU.subtract).then_inc(wqkv_split, 1)
                with pool.Fori(0, NBLK // 2) as i:
                    for p in range(2):
                        for k in range(KK):
                            pool.wait_ge(ht_high[p], FIRST + KK * i + k + 1)
                            nc.gpsimd.tensor_tensor(ht_lo[p][:, k, :], ht[p][:, k, :],
                                                    ht_hi[p][:, k, :].bitcast(F32), ALU.subtract
                                                    ).then_inc(ht_low[p], 1)

            @block.scalar
            def _(act):
                def load(p, i):
                    act.wait_ge(xn_done[p], FIRST + TT * i)
                    src = x[bass.ds((2 * i + p) * TB, TB), :].rearrange("(t p) d -> p t d", p=P)
                    act.dma_start(xin[p][:, :, :], src).then_inc(x_in[p], 16)

                load(0, 0)
                load(1, 0)
                act.wait_ge(setup_in, 48)
                nc.scalar.activation(ce[:, :, :], ct[:, :, :], ACT.Exp, scale=-1.0).then_inc(c_exp, 1)
                nc.scalar.activation(wqkv_hi[:, :, :], wqkv_s[:, :, :], ACT.Copy).then_inc(wqkv_split, 1)
                act.wait_ge(ones_set, 2)

                def part_1(p, i, o):
                    act.wait_ge(qk_mm[p], FIRST + 4 * i + o + 1)
                    if o == 0:
                        act.wait_ge(stored[p], FIRST + 80 * i)
                    nc.scalar.activation(parts[p][:, o, 0, :], bank(2 + o), ACT.Copy).then_inc(part1[p], 1)

                def part_2(p, i, o):
                    act.wait_ge(rest1[p], FIRST + 4 * i + o + 1)
                    nc.scalar.activation(parts[p][:, o, 1, :], rest[:, o, :], ACT.Copy).then_inc(part2[p], 1)

                def values(p, i, half):
                    act.wait_ge(v_mm[p], FIRST + 2 * i + half + 1)
                    nc.scalar.activation(
                        vt[p][:, 2 * half:2 * half + 2, :, 0:DK],
                        bank(6 + half).rearrange("p (t h c) -> p t h c", t=2, h=H), ACT.Copy).then_inc(v_done[p], 1)

                def high_parts(p, i):
                    for k in range(KK):
                        act.wait_ge(ht_done[p], FIRST + KK * i + k + 1)
                        nc.scalar.activation(ht_hi[p][:, k, :], ht[p][:, k, :], ACT.Copy).then_inc(ht_high[p], 1)

                def root(p, i):
                    act.wait_ge(stat_done[p], FIRST + 9 * (i + 1))
                    nc.scalar.activation(rstd[p][:, :], rstd[p][:, :], ACT.Sqrt).then_inc(rooted[p], 1)

                def step(p, i, more=True, ahead=True, loads=True):
                    if loads:
                        load(1 - p, i + p + 1)
                    part_1(p, i, 0)
                    for o in range(1, 4):
                        part_1(p, i, o)
                        part_2(p, i, o - 1)
                        if o == HIGH_AFTER and more:
                            high_parts(*following(p, i))
                    if ahead:
                        root(p, i + 1)
                    part_2(p, i, 3)
                    for half in range(2):
                        values(p, i, half)

                root(0, 0)
                load(0, 1)
                root(1, 0)
                high_parts(0, 0)
                last = NBLK // 2 - 1
                with act.Fori(0, last - 1) as i:
                    for p in range(2):
                        step(p, i)
                step(0, last - 1)
                step(1, last - 1, loads=False)
                step(0, last, ahead=False, loads=False)
                step(1, last, more=False, ahead=False, loads=False)

            @block.vector
            def _(dve):
                dve.wait_ge(c_exp, 1)
                nc.vector.tensor_scalar(ce[:, :, :], ce[:, :, :], 1.0, None, ALU.add).then_inc(c_steps, 1)
                dve.wait_ge(c_steps, 1)
                nc.vector.reciprocal(ce[:, :, :], ce[:, :, :]).then_inc(c_steps, 1)
                dve.wait_ge(c_steps, 2)
                nc.vector.tensor_tensor(silu[:, :, :], ct[:, :, :], ce[:, :, :], ALU.mult).then_inc(c_steps, 1)
                dve.wait_ge(c_steps, 3)
                nc.vector.tensor_copy(silu_all[:, :, :, :], silu[:, :, :].unsqueeze(3).to_broadcast([P, KK, B, P])
                                      ).then_inc(c_steps, 1)

                def gate_guard():
                    dve.wait_ge(gate_mm, 1)
                    g = bank(0, B).rearrange("p (b n) -> p b n", b=B)
                    nc.vector.tensor_scalar(sign[:, :, :], g, 0.0, 2.0, ALU.is_ge, ALU.mult).then_inc(gate_steps, 1)
                    dve.wait_ge(gate_steps, 1)
                    nc.vector.scalar_tensor_tensor(out=size[:, :, :], in0=sign[:, :, :], scalar=1.0, in1=g,
                                                   op0=ALU.subtract, op1=ALU.mult).then_inc(gate_steps, 1)
                    dve.wait_ge(gate_steps, 2)
                    nc.vector.tensor_scalar(size[:, :, :], size[:, :, :], 0.25, None, ALU.max
                                            ).then_inc(gate_steps, 1)
                    dve.wait_ge(gate_steps, 3)
                    nc.vector.scalar_tensor_tensor(out=gates[:, :, :], in0=sign[:, :, :], scalar=1.0,
                                                   in1=size[:, :, :], op0=ALU.subtract, op1=ALU.mult
                                                   ).then_inc(gate_steps, 1)
                    dve.wait_ge(mod_mm, 1)
                    m = bank(4)[:, 0:4 * KK * B].rearrange("p (w k b) -> p w k b", w=4, k=KK)
                    for w in range(4):
                        nc.vector.tensor_scalar(mod_t[:, w], m[:, w], float(w % 2), None, ALU.add
                                                ).then_inc(gate_steps, 1)
                    dve.wait_ge(gate_steps, 8)

                def variance(p, i):
                    dve.wait_ge(x_in[p], FIRST + 16 * (i + 1))
                    for t in range(TT):
                        nc.vector.bn_stats(stats[p][:, t, :], xin[p][:, t, :]).then_inc(stat_done[p], 1)
                    for t in range(TT):
                        wait_apart(dve, stat_done[p], FIRST + 9 * i + t + 1, dve_passed)
                        nc.vector.bn_aggr(mv[p][:, t, :], stats[p][:, t, :]).then_inc(stat_done[p], 1)
                    dve.wait_ge(stat_done[p], FIRST + 9 * i + 8)
                    nc.vector.tensor_scalar(rstd[p][:, :], mv[p][:, :, 1], EPS, None, ALU.add
                                            ).then_inc(stat_done[p], 1)

                def normalise(p, i):
                    dve.wait_ge(rooted[p], FIRST + i + 1)
                    nc.vector.reciprocal(rstd[p][:, :], rstd[p][:, :]).then_inc(inverted[p], 1)
                    dve.wait_ge(inverted[p], FIRST + i + 1)
                    dve.wait_ge(t_mm[p], FIRST + 2 * i)
                    for t in range(TT):
                        nc.vector.tensor_scalar(xn[p][:, t, :], xin[p][:, t, :], mv[p][:, t, 0:1],
                                                rstd[p][:, t:t + 1], ALU.subtract, ALU.mult).then_inc(xn_done[p], 1)

                def modulate(p, i, b):
                    dve.wait_ge(v_mm[p], FIRST + 2 * i)
                    for k in range(KK):
                        dve.wait_ge(t_mm[p], FIRST + 2 * i + k + 1)
                        nc.vector.tensor_scalar(ht[p][:, k, :], bank(k), mod_t[:, 1, k, bass.ds(b, 1)],
                                                mod_t[:, 0, k, bass.ds(b, 1)], ALU.mult, ALU.add
                                                ).then_inc(ht_done[p], 1)

                def rest_1(p, i, o):
                    dve.wait_ge(part1[p], FIRST + 4 * i + o + 1)
                    dve.wait_ge(part3[1 - p], FIRST + 4 * (i + p))
                    nc.vector.tensor_tensor(rest[:, o, :], bank(2 + o), parts[p][:, o, 0, :], ALU.subtract
                                            ).then_inc(rest1[p], 1)

                def part_3(p, i, o):
                    dve.wait_ge(part2[p], FIRST + 4 * i + o + 1)
                    nc.vector.tensor_tensor(parts[p][:, o, 2, :], rest[:, o, :], parts[p][:, o, 1, :], ALU.subtract
                                            ).then_inc(part3[p], 1)

                def step(p, i, b, more=True, ahead=True):
                    rest_1(p, i, 0)
                    if more:
                        modulate(*following(p, i), b)
                    rest_1(p, i, 1)
                    part_3(p, i, 0)
                    if ahead:
                        variance(p, i + 1)
                    rest_1(p, i, 2)
                    part_3(p, i, 1)
                    rest_1(p, i, 3)
                    if ahead:
                        normalise(p, i + 1)
                    part_3(p, i, 2)
                    part_3(p, i, 3)

                variance(0, 0)
                gate_guard()
                normalise(0, 0)
                modulate(0, 0, 0)
                variance(1, 0)
                normalise(1, 0)
                last = NBLK // 2 - 1
                with dve.Fori(0, last) as i:
                    for p in range(2):
                        step(p, i, (i + p) // (BPB // 2))
                step(0, last, B - 1, ahead=False)
                step(1, last, B - 1, more=False, ahead=False)

            @block.tensor
            def _(pe):
                pe.wait_ge(setup_in, 48)
                pe.wait_ge(id_done, 1)
                pe.wait_ge(c_steps, 4)
                for b in range(B):
                    for g, off in ((0, 2 * D), (1, 5 * D)):
                        for k in range(KK):
                            mm = nc.tensor.matmul(bank(b)[:, g * D:(g + 1) * D], silu_all[:, k, b, :],
                                                  wmod_s[:, k, off:off + D], start=(k == 0), stop=(k == KK - 1))
                mm.then_inc(gate_mm, 1)
                for w, which in enumerate((0, 1, 3, 4)):
                    for half in range(KK):
                        for k in range(KK):
                            c0 = which * D + half * P
                            n0 = (w * KK + half) * B
                            mm = nc.tensor.matmul(bank(4)[:, n0:n0 + B], wmod_s[:, k, c0:c0 + P],
                                                  silu[:, k, :], start=(k == 0), stop=(k == KK - 1))
                mm.then_inc(mod_mm, 1)
                pe.wait_ge(gate_steps, 8)
                pe.wait_ge(wqkv_split, 2)

                def transposes(p, i):
                    pe.wait_ge(ht_done[1 - p], FIRST + 2 * (i + p))
                    pe.wait_ge(xn_done[p], FIRST + TT * (i + 1))
                    for k in range(KK):
                        for t in range(TT):
                            mm = nc.tensor.transpose(bank(k)[:, t * P:(t + 1) * P],
                                                     xn[p][:, t, k * P:(k + 1) * P], ident[:, :])
                        mm.then_inc(t_mm[p], 1)

                def queries_keys(p, i, outputs):
                    if outputs[0] == 0:
                        pe.wait_ge(rest1[1 - p], FIRST + 4 * (i + p))
                        pe.wait_ge(ht_high[p], FIRST + KK * (i + 1))
                    for o in outputs:
                        cols = slice(o * P, (o + 1) * P)
                        for k in range(KK):
                            nc.tensor.matmul(bank(2 + o), wqkv_hi[:, k, cols], ht_hi[p][:, k, :],
                                             start=(k == 0), stop=False)
                            nc.tensor.matmul(bank(2 + o), wqkv_lo[:, k, cols], ht_hi[p][:, k, :],
                                             start=False, stop=False)
                        for k in range(KK):
                            if o == 0:
                                pe.wait_ge(ht_low[p], FIRST + KK * i + k + 1)
                            mm = nc.tensor.matmul(bank(2 + o), wqkv_hi[:, k, cols], ht_lo[p][:, k, :],
                                                  start=False, stop=(k == KK - 1))
                        mm.then_inc(qk_mm[p], 1)

                def values(p, i):
                    pe.wait_ge(v_done[1 - p], FIRST + 2 * (i + p))
                    for t in range(TT):
                        o = bank(6 + t // 2)[:, (t % 2) * D:(t % 2 + 1) * D]
                        for k in range(KK):
                            hi, lo = (h[p][:, k, t * P:(t + 1) * P] for h in (ht_hi, ht_lo))
                            nc.tensor.matmul(o, hi, wqkv_hi[:, k, 2 * D:3 * D], start=(k == 0), stop=False)
                            nc.tensor.matmul(o, hi, wqkv_lo[:, k, 2 * D:3 * D], start=False, stop=False)
                            mm = nc.tensor.matmul(o, lo, wqkv_hi[:, k, 2 * D:3 * D],
                                                  start=False, stop=(k == KK - 1))
                        if t % 2:
                            mm.then_inc(v_mm[p], 1)

                def step(p, i, more=True):
                    queries_keys(p, i, range(QK_BEFORE))
                    if more:
                        transposes(*following(p, i))
                    queries_keys(p, i, range(QK_BEFORE, 4))
                    values(p, i)

                transposes(0, 0)
                last = NBLK // 2 - 1
                with pe.Fori(0, last) as i:
                    for p in range(2):
                        step(p, i)
                step(0, last)
                step(1, last, more=False)


def block2(nc, sb_, sem, sems, counts, bank, q_parts, k_parts, v_ones, contexts, ident):
    with ExitStack() as own:
        def sb(name, shape, dt=F32):
            return sb_(name, shape, dt, own)

        qs = [sb(f"qs{p}", [STACK + PARTS, HG, S], BF16) for p in range(2)]
        ks = [sb(f"ks{p}", [STACK + PARTS, HG, S], BF16) for p in range(2)]
        vs = [sb(f"vs{p}", [P, QT, HG, VW]) for p in range(2)]
        probs = [sb(f"probs{k}", [P, HG, TB]) for k in range(PB)]
        causal = sb("causal", [P, CW])
        causal_b = sb("causal_b", [P, P], BF16)
        ident_b = sb("ident_b", [P, P], BF16)
        junk = [sb(f"junk{k}", [P, CW], BF16) for k in range(2)]
        maxima = [sb(f"maxima{p}", [P, HG, QT]) for p in range(2)]
        early = sb("early", [P, HG, QT, (S - 1) // CW])
        early_max = sb("early_max", [P, HG, QT])
        neg = [sb(f"neg{p}", [HG * QT, PARTS, P], BF16) for p in range(2)]
        neg_rest = sb("neg_rest", [HG * QT, P])
        ctx_out = [sb(f"ctx_out{k}", [P, TB]) for k in range(2)]

        causal_set = sem("causal_set")
        mask_set = sem("mask_set")
        ones_set = sem("k_ones_set")
        heads_in = [sems(f"heads_in{p}_", HG) for p in range(2)]
        v_in = sems("v_in")
        max_mm, max_done = sems("max_mm"), sems("max_done")
        joined = sems("joined")
        max_all, max_t = sems("max_all"), sems("max_t")
        neg_done, neg_in = sems("neg_done"), sems("neg_in")
        s_mm, exp_done = sems("s_mm"), sems("exp_done")
        pv_mm, ctx_done = sems("pv_mm"), sems("ctx_done")
        ctx_stored = sems("ctx_stored")
        last = NG // 2 - 1

        def place(p, i):
            per = B * H // HG // B
            return (2 * i + p) // per if isinstance(i, int) else i // (per // 2), (i % (per // 2)) * 2 + p

        sp_passed, dve_passed, pe_passed = (sem(f"{n}_passed_a") for n in ("sp", "dve", "pe"))
        count_from_first(nc, counts)
        with nc.Block() as block:
            @block.sync
            def _(sp):
                def load(p, i):
                    b, hg = place(p, i)
                    wait_apart(sp, s_mm[p], FIRST + NS * i, sp_passed)
                    for h in range(HG):
                        rows = bass.ds((hg * HG + h) * DK, DK)
                        toks = bass.ds(b * S, S)
                        for side, src, same in ((qs[p], q_parts, False), (ks[p], k_parts, True)):
                            for r0, n, other in ((0, 3, 0), (3 * DK, 2, 1), (5 * DK, 1, 2)):
                                if same:
                                    s = src[rows, other:other + 1, toks].to_broadcast([DK, n, S])
                                else:
                                    s = src[rows, 0:n, toks]
                                sp.dma_start(side[r0:r0 + n * DK, h, :], s).then_inc(heads_in[p][h], 16)

                def load_v(p, i):
                    b, hg = place(p, i)
                    wait_apart(sp, pv_mm[p], FIRST + NU * i, sp_passed)
                    src = v_ones[bass.ds(b * S, S), bass.ds(hg * (HG * VW), HG * VW)]
                    sp.dma_start(vs[p][:, :, :, :].rearrange("p t h c -> p t (h c)"),
                                 src.rearrange("(t p) c -> p t c", p=P)).then_inc(v_in[p], 16)

                def store(p, i, j):
                    b, hg = place(p, i)
                    wait_apart(sp, ctx_done[p], FIRST + BPB * i + j + 1, sp_passed)
                    sp.dma_start(contexts[bass.ds(hg * P, P), bass.ds(b * S + j * TB, TB)],
                                 ctx_out[j % 2][:, :]).then_inc(ctx_stored[j % 2], 16)

                def put_neg(p, i):
                    wait_apart(sp, neg_done[p], FIRST + 4 * (i + 1), sp_passed)
                    for n in range(PARTS):
                        sp.dma_start(qs[p][STACK + n:STACK + n + 1, :, :].rearrange("a h (t c) -> a (h t) c", c=P),
                                     neg[p][:, n, :]).then_inc(neg_in[p], 16)

                def step(p, i, before=True, more=True):
                    if more:
                        load(*following(p, i))
                    if before:
                        store(*preceding(p, i), BPB - 1)
                    if more:
                        load_v(*following(p, i))
                    for j in range(BPB - 1):
                        store(p, i, j)
                    if more:
                        put_neg(*following(p, i))

                load(0, 0)
                load_v(0, 0)
                put_neg(0, 0)
                step(0, 0, before=False)
                with sp.Fori(0, last) as i:
                    step(1, i)
                    step(0, i + 1)
                step(1, last, more=False)
                store(1, last, BPB - 1)
                for k in range(2):
                    sp.wait_ge(ctx_stored[k], FIRST + 16 * NG * BPB // 2)

            @block.gpsimd
            def _(pool):
                nc.gpsimd.memset(causal[:, :], 0.0).then_inc(causal_set, 1)
                pool.wait_ge(causal_set, 1)
                nc.gpsimd.affine_select(out=causal[:, CW - P:CW], in_=causal[:, CW - P:CW], compare_op=ALU.is_ge,
                                        fill=NEG, base=0, pattern=[[-1, P]], channel_multiplier=1
                                        ).then_inc(causal_set, 1)
                pool.wait_ge(causal_set, 2)
                for p in range(2):
                    pool.wait_ge(ones_set, p)
                    nc.gpsimd.memset(ks[p][STACK:STACK + PARTS, :, :], 1.0).then_inc(ones_set, 1)

            @block.scalar
            def _(act):
                def context(p, i, j):
                    act.wait_ge(pv_mm[p], FIRST + NU * i + UNITS_TO[j])
                    act.wait_ge(ctx_stored[j % 2], FIRST + 16 * (4 * i + 2 * p + j // 2))
                    nc.scalar.activation(ctx_out[j % 2][:, :], bank(3), ACT.Copy).then_inc(ctx_done[p], 1)

                def step(p, i, before=True):
                    for u, (j, kt, q0) in enumerate(UNITS):
                        if u >= PB:
                            act.wait_ge(pv_mm[p], FIRST + NU * i + u - PB + 1)
                        elif before:
                            act.wait_ge(pv_mm[1 - p], FIRST + NU * (i + p) + u - PB + 1)
                        for h in range(HG):
                            if h == 2 and u == LAG - 1 and before:
                                context(*preceding(p, i), BPB - 1)
                            if h == 2 and u - LAG + 1 in UNITS_TO:
                                context(p, i, UNITS_TO.index(u - LAG + 1))
                            n = HG * u + h
                            act.wait_ge(s_mm[p], FIRST + NS * i + n + 1)
                            nc.scalar.activation(probs[u % PB][:, h, q0:TB], bank(n % SB)[:, q0:TB], ACT.Exp,
                                                 scale=SCALE).then_inc(exp_done[p], 1)

                step(0, 0, before=False)
                with act.Fori(0, last) as i:
                    step(1, i)
                    step(0, i + 1)
                step(1, last)
                context(1, last, BPB - 1)

            @block.vector
            def _(dve):
                dve.wait_ge(causal_set, 2)
                nc.vector.memset(early[:, :, :, :], -3e38).then_inc(mask_set, 1)
                dve.wait_ge(mask_set, 1)
                nc.vector.tensor_copy(causal_b[:, :], causal[:, CW - P:CW]).then_inc(mask_set, 1)
                nc.vector.tensor_copy(ident_b[:, :], ident[:, :]).then_inc(mask_set, 1)

                def maxima_of(p, i):
                    for c, (h, t, k0, w, end) in enumerate(CHUNKS):
                        if c >= 2:
                            dve.wait_ge(max_done[p], FIRST + NC * i + c - 1)
                        wait_apart(dve, max_mm[p], FIRST + NC * i + c + 1, dve_passed)
                        tile = bank(4 + c % MS * (CW // 512), CW // 512)[:, 0:w]
                        if end:
                            nc.vector.tensor_tensor_reduce(
                                junk[c % 2][:, 0:w], tile, causal[:, CW - w:CW], 1.0, -3e38, ALU.add, ALU.max,
                                maxima[p][:, h, t:t + 1]).then_inc(max_done[p], 1)
                        else:
                            nc.vector.tensor_reduce(early[:, h, t, k0 // CW:k0 // CW + 1], tile, AX.X, ALU.max
                                                    ).then_inc(max_done[p], 1)
                    dve.wait_ge(max_done[p], FIRST + NC * (i + 1))
                    nc.vector.tensor_reduce(early_max[:, :, :], early[:, :, :, :], AX.X, ALU.max
                                            ).then_inc(joined[p], 1)
                    dve.wait_ge(joined[p], FIRST + i + 1)
                    nc.vector.tensor_tensor(maxima[p][:, :, :], maxima[p][:, :, :], early_max[:, :, :], ALU.max
                                            ).then_inc(max_all[p], 1)
                    dve.wait_ge(max_t[p], FIRST + i + 1)
                    dve.wait_ge(neg_in[p], FIRST + 48 * i)
                    m = bank(4)[0:HG * QT, 0:P]
                    nc.vector.tensor_scalar(neg[p][:, 0, :], m, -1.0, None, ALU.mult).then_inc(neg_done[p], 1)
                    dve.wait_ge(neg_done[p], FIRST + 4 * i + 1)
                    nc.vector.scalar_tensor_tensor(out=neg_rest[:, :], in0=m, scalar=-1.0, in1=neg[p][:, 0, :],
                                                   op0=ALU.mult, op1=ALU.subtract).then_inc(neg_done[p], 1)
                    dve.wait_ge(neg_done[p], FIRST + 4 * i + 2)
                    nc.vector.tensor_copy(neg[p][:, 1, :], neg_rest[:, :]).then_inc(neg_done[p], 1)
                    dve.wait_ge(neg_done[p], FIRST + 4 * i + 3)
                    nc.vector.tensor_tensor(neg[p][:, 2, :], neg_rest[:, :], neg[p][:, 1, :], ALU.subtract
                                            ).then_inc(neg_done[p], 1)

                maxima_of(0, 0)
                with dve.Fori(0, last) as i:
                    for p in range(2):
                        maxima_of(*following(p, i))
                maxima_of(1, last)

            @block.tensor
            def _(pe):
                pe.wait_ge(ones_set, 2)
                pe.wait_ge(mask_set, 3)

                def max_chunk(p, i, c):
                    h, t, k0, w, _ = CHUNKS[c]
                    if c == 0 or CHUNKS[c - 1][0] != h:
                        pe.wait_ge(heads_in[p][h], FIRST + 96 * (i + 1))
                    if c >= MS:
                        pe.wait_ge(max_done[p], FIRST + NC * i + c - MS + 1)
                    elif c == 0:
                        pe.wait_ge(neg_done[1 - p], FIRST + 4 * (i + p))
                    for m0 in range(0, w, 512):
                        n = min(512, w - m0)
                        mm = nc.tensor.matmul(bank(4 + c % MS * (CW // 512), CW // 512)[:, m0:m0 + n],
                                              qs[p][0:STACK, h, t * P:(t + 1) * P],
                                              ks[p][0:STACK, h, k0 + m0:k0 + m0 + n], start=True, stop=True)
                    mm.then_inc(max_mm[p], 1)

                def max_turn(p, i):
                    wait_apart(pe, max_all[p], FIRST + i + 1, pe_passed)
                    nc.tensor.transpose(bank(4)[0:HG * QT, 0:P], maxima[p][:, :, :].rearrange("p h t -> p (h t)"),
                                        ident[:, :]).then_inc(max_t[p], 1)

                def score(p, i, u, h):
                    j, kt, q0 = UNITS[u]
                    n = HG * u + h
                    if n == 0:
                        pe.wait_ge(neg_in[p], FIRST + 48 * (i + 1))
                        pe.wait_ge(exp_done[1 - p], FIRST + NS * (i + p))
                    elif n >= SB:
                        pe.wait_ge(exp_done[p], FIRST + NS * i + n - SB + 1)
                    mm = nc.tensor.matmul(bank(n % SB)[:, q0:TB], ks[p][:, h, kt * P:(kt + 1) * P],
                                          qs[p][:, h, j * TB + q0:(j + 1) * TB], start=True, stop=not DIAG[u])
                    if DIAG[u]:
                        mm = nc.tensor.matmul(bank(n % SB)[:, q0:q0 + P], causal_b[:, :], ident_b[:, :],
                                              start=False, stop=True)
                    mm.then_inc(s_mm[p], 1)

                def p_v(p, i, u):
                    j, kt, q0 = UNITS[u]
                    if u == 0:
                        pe.wait_ge(v_in[p], FIRST + 16 * (i + 1))
                        pe.wait_ge(ctx_done[1 - p], FIRST + BPB * (i + p))
                    elif kt == 0:
                        pe.wait_ge(ctx_done[p], FIRST + BPB * i + j)
                    pe.wait_ge(exp_done[p], FIRST + NS * i + HG * (u + 1))
                    for h in range(HG):
                        mm = nc.tensor.matmul(bank(3)[VW * h:VW * (h + 1), q0:TB], vs[p][:, kt, h, :],
                                              probs[u % PB][:, h, q0:TB], start=(kt == 0),
                                              stop=(kt == TT * (j + 1) - 1))
                    mm.then_inc(pv_mm[p], 1)

                def step(p, i, before=True, more=True):
                    def chunks(n):
                        if more:
                            for c in PLAN[n]:
                                max_chunk(*following(p, i), c)

                    for u in range(NU):
                        score(p, i, u, 0)
                        chunks(POINTS * u)
                        score(p, i, u, 1)
                        chunks(POINTS * u + 1)
                        if u >= LAG:
                            p_v(p, i, u - LAG)
                        elif before:
                            p_v(*preceding(p, i), NU - LAG + u)
                        chunks(POINTS * u + 2)
                        score(p, i, u, 2)
                        chunks(POINTS * u + 3)
                        score(p, i, u, 3)
                        chunks(POINTS * u + 4)
                        if more and u == PLAN_LAST + 1:
                            max_turn(*following(p, i))

                for c in range(NC):
                    max_chunk(0, 0, c)
                max_turn(0, 0)
                step(0, 0, before=False)
                with pe.Fori(0, last) as i:
                    step(1, i)
                    step(0, i + 1)
                step(1, last, more=False)
                for u in range(NU - LAG, NU):
                    p_v(1, last, u)


def block3(nc, sb_, sem, sems, counts, bank, x, contexts, w1, w2, wo_s, rw_s, ident, mod_t, gates, w_in, out):
    with ExitStack() as own:
        def sb(name, shape, dt=F32):
            return sb_(name, shape, dt, own)

        num = [sb(f"num{p}", [P, KK, TB]) for p in range(2)]
        den = [sb(f"den{p}", [P, KK, TB]) for p in range(2)]
        xres = [sb(f"xres{p}", [P, TT, D]) for p in range(2)]
        gated = sb("gated", [P, TT, D])
        stats = sb("stats_b", [P, TT, 6])
        mv = sb("mv_b", [P, TT, 2])
        rstd = sb("rstd_b", [P, TT])
        xn = sb("xn_b", [P, TT, D])
        h2t = sb("h2t", [P, KK, TB])
        h2_hi = [sb(f"h2_hi{p}", [P, KK, TB], F32R) for p in range(2)]
        h2_lo = [sb(f"h2_lo{p}", [P, KK, TB], F32R) for p in range(2)]
        w1_hi, w1_lo = (sb(f"w1_{n}", [P, KK, NW * P], F32R) for n in ("hi", "lo"))
        w2_hi, w2_lo = (sb(f"w2_{n}", [P, NW, D], F32R) for n in ("hi", "lo"))
        stage = [sb(f"stage{k}", [P, NW * P // 2]) for k in range(2)]
        gate_e = sb("gate_e", [P, TT, E])
        prob = sb("prob", [P, TT, E])
        rank = sb("rank", [P, TT, E])
        beats = sb("beats", [P, TT, E])
        top = sb("top", [P, TT, E])
        top_sum = sb("top_sum", [P, TT])
        combine = [sb(f"combine{p}", [P, TT, E]) for p in range(2)]
        hid, relu = ([s[:, k * TB:(k + 1) * TB] for k in range(HF - 1)] + [sb(name, [P, TB])]
                     for s, name in zip(stage, ("hid", "relu")))
        hid_hi = [sb(f"hid_hi{k}", [P, TB], F32R) for k in range(HB)]
        hid_lo = [sb(f"hid_lo{k}", [P, TB], F32R) for k in range(HB)]
        mix = [sb(f"mix{p}", [P, TT, D]) for p in range(2)]
        res = [sb(f"res{p}", [P, TT, D]) for p in range(2)]

        ctx_in, x_in = sems("ctx_in"), sems("xres_in")
        den_inv, ctx_norm = sems("den_inv"), sems("ctx_norm")
        rooted, inverted = sems("rooted_b"), sems("inverted_b")
        o_mm, res_done, ln_steps = sems("o_mm"), sems("res_done"), sems("ln_steps")
        t_mm, h_done = sems("t2_mm"), sems("h2_done")
        r_mm, r_exp, r_steps = sems("r_mm"), sems("r_exp"), sems("r_steps")
        hi_done, lo_done = sems("hi_done"), sems("lo_done")
        h_hi, h_lo = sems("h_hi"), sems("h_lo")
        w_hi = sem("w_hi")
        w_lo = [sem(f"w_lo{k}") for k in range(2)]
        stage_in = [sem(f"stage_in{k}") for k in range(2)]
        pool_lo = sems("pool_lo")
        u_mm, relu_done, hid_done, d_mm = sems("u_mm"), sems("relu_done"), sems("hid_done"), sems("d_mm")
        mix_done, final, out_done = sems("mix_done"), sems("final"), sems("out_done")
        last = NBLK // 2 - 1
        pieces = []
        for k in range(KK):
            for half in range(2):
                cols = slice(half * NW * P // 2, (half + 1) * NW * P // 2)
                pieces.append((w1[k * P:(k + 1) * P, cols], w1_hi[:, k, cols], w1_lo[:, k, cols]))
        for k in range(4):
            tiles = slice(k * NW // 4, (k + 1) * NW // 4)
            pieces.append((w2[k * NW // 4 * P:(k + 1) * NW // 4 * P, :].rearrange("(t p) n -> p t n", p=P),
                           w2_hi[:, tiles, :], w2_lo[:, tiles, :]))

        def staged(q):
            s = stage[q % 2][:, :]
            return s if q < 4 else s.rearrange("p (t n) -> p t n", n=D)

        RS = 3 + 2 * E + 5

        def batch(p, i):
            return (2 * i + p) // BPB if isinstance(i, int) else i // (BPB // 2)

        sp_passed, dve_passed = sem("sp_passed_b"), sem("dve_passed_b")
        count_from_first(nc, counts)
        def low_weights(engine, ops, q):
            _, hi, lo = pieces[q]
            engine.wait_ge(w_hi, q + 1)
            ops.tensor_tensor(lo, staged(q), hi.bitcast(F32), ALU.subtract).then_inc(w_lo[q % 2], 1)

        def low_part(engine, ops, p, i, w):
            engine.wait_ge(hi_done[p], FIRST + NW * i + w + 1)
            which = lo_done[p] if w not in POOL_LO else pool_lo[p]
            ops.tensor_tensor(hid_lo[w % HB][:, :], hid[w % HF][:, :], hid_hi[w % HB][:, :].bitcast(F32),
                              ALU.subtract).then_inc(which, 1)

        def low_parts_done(engine, p, i, w):
            on_pool = sum(v in POOL_LO for v in range(w + 1))
            engine.wait_ge(lo_done[p], FIRST + (NW - len(POOL_LO)) * i + w + 1 - on_pool)
            engine.wait_ge(pool_lo[p], FIRST + len(POOL_LO) * i + on_pool)

        with nc.Block() as block:
            @block.sync
            def _(sp):
                sp.wait_ge(w_in, 32)

                def load_contexts(p, i):
                    n = 2 * i + p
                    wait_apart(sp, o_mm[p], FIRST + TT * i, sp_passed)
                    cols = bass.ds(n * TB, TB)
                    for k in range(KK):
                        rows = contexts[k * H // KK * VW:(k + 1) * H // KK * VW, cols].rearrange(
                            "(h c) t -> h c t", c=VW)
                        sp.dma_start(num[p][:, k, :], rows[:, 0:DK, :]).then_inc(ctx_in[p], 16)
                        sp.dma_start(den[p][:, k, :], rows[:, DK:VW, :]).then_inc(ctx_in[p], 16)

                def load_x(p, i):
                    cols = bass.ds((2 * i + p) * TB, TB)
                    wait_apart(sp, final[p], FIRST + 2 * TT * i, sp_passed)
                    sp.dma_start(xres[p][:, :, :], x[cols, :].rearrange("(t p) d -> p t d", p=P)
                                 ).then_inc(x_in[p], 16)

                def store(p, i):
                    wait_apart(sp, final[p], FIRST + 2 * TT * (i + 1), sp_passed)
                    sp.dma_start(out[bass.ds((2 * i + p) * TB, TB), :].rearrange("(t p) d -> p t d", p=P),
                                 res[p][:, :, :]).then_inc(out_done[p], 16)

                def load_piece(q):
                    if q >= 2:
                        sp.wait_ge(w_lo[q % 2], q // 2)
                    sp.dma_start(staged(q), pieces[q][0]).then_inc(stage_in[q % 2], 16)

                load_contexts(0, 0)
                load_piece(0)
                load_x(0, 0)
                load_piece(1)
                load_piece(2)
                load_piece(3)
                load_contexts(1, 0)
                load_x(1, 0)
                for q in range(4, 8):
                    load_piece(q)
                with sp.Fori(0, last) as i:
                    for p in range(2):
                        load_contexts(p, i + 1)
                        store(p, i)
                        load_x(p, i + 1)
                for p in range(2):
                    store(p, last)
                for p in range(2):
                    sp.wait_ge(out_done[p], FIRST + 16 * (last + 1))

            @block.gpsimd
            def _(pool):
                for q in range(0, len(pieces), 2):
                    low_weights(pool, nc.gpsimd, q)

                def out_tokens(p, i):
                    b = batch(p, i)
                    pool.wait_ge(out_done[p], FIRST + 16 * i)
                    pool.wait_ge(mix_done[p], FIRST + TT * E * (i + 1))
                    for t in range(TT):
                        nc.gpsimd.tensor_tensor(res[p][:, t, :], mix[p][:, t, :],
                                                gates[:, bass.ds(b, 1), D:2 * D].squeeze(1), ALU.mult
                                                ).then_inc(final[p], 1)
                    for t in range(TT):
                        pool.wait_ge(final[p], FIRST + 2 * TT * i + t + 1)
                        nc.gpsimd.tensor_tensor(res[p][:, t, :], res[p][:, t, :], xres[p][:, t, :], ALU.add
                                                ).then_inc(final[p], 1)

                def step(p, i, first=False):
                    for w in POOL_LO:
                        low_part(pool, nc.gpsimd, p, i, w)
                        if w == POOL_LO[OUT_AT] and not first:
                            out_tokens(*preceding(p, i))

                step(0, 0, first=True)
                with pool.Fori(0, last) as i:
                    step(1, i)
                    step(0, i + 1)
                step(1, last)
                out_tokens(1, last)

            @block.scalar
            def _(act):
                def router_exp(p, i):
                    act.wait_ge(r_mm[p], FIRST + i + 1)
                    act.wait_ge(r_steps[1 - p], FIRST + RS * (i + p))
                    nc.scalar.activation(gate_e[:, :, :], bank(6)[:, 0:TT * E].rearrange("p (t e) -> p t e", e=E),
                                         ACT.Exp, scale=-1.0).then_inc(r_exp[p], 1)

                def root(p, i):
                    act.wait_ge(ln_steps[p], FIRST + (4 * TT + 1) * (i + 1))
                    nc.scalar.activation(rstd[:, :], rstd[:, :], ACT.Sqrt).then_inc(rooted[p], 1)

                def high_h2(p, i):
                    act.wait_ge(h_done[p], FIRST + KK * (i + 1))
                    act.wait_ge(u_mm[p], FIRST + NW * i)
                    nc.scalar.activation(h2_hi[p][:, :, :], h2t[:, :, :], ACT.Copy).then_inc(h_hi[p], 1)

                def step(p, i, first=False, more=True):
                    for w in range(NW + 1):
                        if w < NW:
                            act.wait_ge(u_mm[p], FIRST + NW * i + w + 1)
                            if w >= HF:
                                act.wait_ge(hid_done[p], FIRST + NW * i + w - HF + 1)
                            elif not first:
                                act.wait_ge(hid_done[1 - p], FIRST + NW * (i + p) + w - HF + 1)
                            nc.scalar.activation(relu[w % HF][:, :], bank(w % 2), ACT.Relu).then_inc(relu_done[p], 1)
                        if w >= 1:
                            v = w - 1
                            act.wait_ge(hid_done[p], FIRST + NW * i + v + 1)
                            if v >= HB:
                                act.wait_ge(d_mm[p], FIRST + NW * i + v - HB + 1)
                            elif not first:
                                act.wait_ge(d_mm[1 - p], FIRST + NW * (i + p) + v - HB + 1)
                            nc.scalar.activation(hid_hi[v % HB][:, :], hid[v % HF][:, :], ACT.Copy
                                                 ).then_inc(hi_done[p], 1)
                        if w == STATISTICS and more:
                            root(*following(p, i))
                        if w == MODULATE and more:
                            high_h2(*following(p, i))
                        if w == ROUTE + 1 and more:
                            router_exp(*following(p, i))

                def high_weights(q):
                    act.wait_ge(stage_in[q % 2], 16 * (q // 2 + 1))
                    nc.scalar.activation(pieces[q][1], staged(q), ACT.Copy).then_inc(w_hi, 1)

                for q in range(4):
                    high_weights(q)
                root(0, 0)
                high_weights(4)
                high_h2(0, 0)
                high_weights(5)
                router_exp(0, 0)
                high_weights(6)
                high_weights(7)
                step(0, 0, first=True)
                with act.Fori(0, last) as i:
                    step(1, i)
                    step(0, i + 1)
                step(1, last, more=False)

            @block.vector
            def _(dve):
                def inverse_denominators(p, i, quarter):
                    if quarter == 0:
                        dve.wait_ge(ctx_in[p], FIRST + 64 * (i + 1))
                    k, half = quarter // 2, slice(quarter % 2 * TB // 2, (quarter % 2 + 1) * TB // 2)
                    nc.vector.reciprocal(den[p][:, k, half], den[p][:, k, half]).then_inc(den_inv[p], 1)

                def contexts_over_denominators(p, i):
                    dve.wait_ge(den_inv[p], FIRST + 4 * (i + 1))
                    nc.vector.tensor_tensor(num[p][:, :, :], num[p][:, :, :], den[p][:, :, :], ALU.mult
                                            ).then_inc(ctx_norm[p], 1)

                def gate_attention(p, i, b):
                    for t in range(TT):
                        dve.wait_ge(o_mm[p], FIRST + TT * i + 2 * (t // 2) + 2)
                        nc.vector.tensor_tensor(gated[:, t, :], bank(6 + t // 2)[:, (t % 2) * D:(t % 2 + 1) * D],
                                                gates[:, bass.ds(b, 1), 0:D].squeeze(1), ALU.mult
                                                ).then_inc(ln_steps[p], 1)

                def residual(p, i):
                    dve.wait_ge(x_in[p], FIRST + 16 * (i + 1))
                    dve.wait_ge(t_mm[1 - p], FIRST + KK * (i + p))
                    n = 4 * TT + 1
                    for t in range(TT):
                        dve.wait_ge(ln_steps[p], FIRST + n * i + t + 1)
                        nc.vector.tensor_tensor(xres[p][:, t, :], gated[:, t, :], xres[p][:, t, :], ALU.add
                                                ).then_inc(ln_steps[p], 1)

                def statistics(p, i):
                    n = 4 * TT + 1
                    for t in range(TT):
                        dve.wait_ge(ln_steps[p], FIRST + n * i + TT + t + 1)
                        nc.vector.bn_stats(stats[:, t, :], xres[p][:, t, :]).then_inc(ln_steps[p], 1)
                    for t in range(TT):
                        wait_apart(dve, ln_steps[p], FIRST + n * i + 2 * TT + t + 1, dve_passed)
                        nc.vector.bn_aggr(mv[:, t, :], stats[:, t, :]).then_inc(ln_steps[p], 1)
                    dve.wait_ge(ln_steps[p], FIRST + n * i + 4 * TT)
                    nc.vector.tensor_scalar(rstd[:, :], mv[:, :, 1], EPS, None, ALU.add
                                            ).then_inc(ln_steps[p], 1)

                def normalise(p, i):
                    dve.wait_ge(rooted[p], FIRST + i + 1)
                    nc.vector.reciprocal(rstd[:, :], rstd[:, :]).then_inc(inverted[p], 1)
                    dve.wait_ge(inverted[p], FIRST + i + 1)
                    for t in range(TT):
                        nc.vector.tensor_scalar(xn[:, t, :], xres[p][:, t, :], mv[:, t, 0:1], rstd[:, t:t + 1],
                                                ALU.subtract, ALU.mult).then_inc(res_done[p], 1)

                def modulate(p, i, b):
                    dve.wait_ge(r_mm[1 - p], FIRST + i + p)
                    dve.wait_ge(h_hi[1 - p], FIRST + i + p)
                    for k in range(KK):
                        dve.wait_ge(t_mm[p], FIRST + KK * i + k + 1)
                        nc.vector.tensor_scalar(h2t[:, k, :], bank(6 + k), mod_t[:, 3, k, bass.ds(b, 1)],
                                                mod_t[:, 2, k, bass.ds(b, 1)], ALU.mult, ALU.add
                                                ).then_inc(h_done[p], 1)

                def low_h2(p, i):
                    dve.wait_ge(h_hi[p], FIRST + i + 1)
                    nc.vector.tensor_tensor(h2_lo[p][:, :, :], h2t[:, :, :], h2_hi[p][:, :, :].bitcast(F32),
                                            ALU.subtract).then_inc(h_lo[p], 1)

                def linked(p, i, step, ins):
                    ins.then_inc(r_steps[p], 1)
                    dve.wait_ge(r_steps[p], FIRST + RS * i + step)

                def probabilities(p, i):
                    dve.wait_ge(r_exp[p], FIRST + i + 1)
                    linked(p, i, 1, nc.vector.tensor_scalar(gate_e[:, :, :], gate_e[:, :, :], 1.0, None, ALU.add))
                    linked(p, i, 2, nc.vector.reciprocal(prob[:, :, :], gate_e[:, :, :]))
                    linked(p, i, 3, nc.vector.memset(rank[:, :, :], 0.0))

                def rank_of(p, i, experts):
                    for e in experts:
                        one = prob[:, :, e:e + 1]
                        beaten = nc.vector.tensor_tensor(beats[:, :, 0:e + 1], one.to_broadcast([P, TT, e + 1]),
                                                         prob[:, :, 0:e + 1], ALU.is_gt)
                        if e + 1 < E:
                            beaten = nc.vector.tensor_tensor(
                                beats[:, :, e + 1:E], one.to_broadcast([P, TT, E - e - 1]),
                                prob[:, :, e + 1:E], ALU.is_ge)
                        linked(p, i, 4 + 2 * e, beaten)
                        linked(p, i, 5 + 2 * e, nc.vector.tensor_tensor(rank[:, :, :], rank[:, :, :],
                                                                        beats[:, :, :], ALU.add))

                def shares(p, i):
                    dve.wait_ge(mix_done[p], FIRST + TT * E * i)
                    n = 3 + 2 * E
                    linked(p, i, n + 1, nc.vector.scalar_tensor_tensor(out=top[:, :, :], in0=rank[:, :, :], scalar=2.0,
                                                                       in1=prob[:, :, :], op0=ALU.is_lt, op1=ALU.mult))
                    linked(p, i, n + 2, nc.vector.tensor_reduce(top_sum[:, :], top[:, :, :], AX.X, ALU.add))
                    linked(p, i, n + 3, nc.vector.tensor_scalar(top_sum[:, :], top_sum[:, :], 1e-20, None, ALU.add))
                    linked(p, i, n + 4, nc.vector.reciprocal(top_sum[:, :], top_sum[:, :]))
                    linked(p, i, n + 5, nc.vector.tensor_tensor(combine[p][:, :, :], top[:, :, :],
                                                                top_sum[:, :].unsqueeze(2).to_broadcast([P, TT, E]),
                                                                ALU.mult))

                def hidden(p, i, w, first):
                    dve.wait_ge(relu_done[p], FIRST + NW * i + w + 1)
                    if w >= HF:
                        low_parts_done(dve, p, i, w - HF)
                    elif not first:
                        low_parts_done(dve, 1 - p, i + p - 1, NW + w - HF)
                    nc.vector.tensor_tensor(hid[w % HF][:, :], relu[w % HF][:, :], relu[w % HF][:, :], ALU.mult
                                            ).then_inc(hid_done[p], 1)

                def mixed(p, i, e):
                    dve.wait_ge(d_mm[p], FIRST + NW * i + FIRST_W[e] + FT[e])
                    if e == 0:
                        dve.wait_ge(final[p], FIRST + 2 * TT * i)
                    for t in range(TT):
                        y = bank(2 + 2 * (e % 2) + t // 2)[:, (t % 2) * D:(t % 2 + 1) * D]
                        share = combine[p][:, t, e:e + 1]
                        if e == 0:
                            nc.vector.tensor_scalar(mix[p][:, t, :], y, share, None, ALU.mult
                                                    ).then_inc(mix_done[p], 1)
                        else:
                            dve.wait_ge(mix_done[p], FIRST + TT * E * i + TT * (e - 1) + t + 1)
                            nc.vector.scalar_tensor_tensor(out=mix[p][:, t, :], in0=y, scalar=share,
                                                           in1=mix[p][:, t, :], op0=ALU.mult, op1=ALU.add
                                                           ).then_inc(mix_done[p], 1)

                def step(p, i, first=False, more=True):
                    nxt = following(p, i)
                    for w in range(NW + 1):
                        if w < NW:
                            hidden(p, i, w, first)
                        if w >= 1 and w - 1 not in POOL_LO:
                            low_part(dve, nc.vector, p, i, w - 1)
                        if w == MIX_LAG - 1 and not first:
                            mixed(*preceding(p, i), E - 1)
                        if w >= MIX_LAG and EXPERT[w - MIX_LAG] != EXPERT[w - MIX_LAG + 1]:
                            mixed(p, i, EXPERT[w - MIX_LAG])
                        if not more:
                            continue
                        if w in INVERSE:
                            inverse_denominators(*nxt, INVERSE.index(w))
                        if w == CONTEXTS:
                            contexts_over_denominators(*nxt)
                        if w == GATE:
                            gate_attention(*nxt, batch(*nxt))
                        if w == RESIDUAL:
                            residual(*nxt)
                        if w == STATISTICS:
                            statistics(*nxt)
                        if w == NORMALISE:
                            normalise(*nxt)
                        if w == MODULATE:
                            modulate(*nxt, batch(*nxt))
                        if w == LOW:
                            low_h2(*nxt)
                        if w == ROUTE + 2:
                            probabilities(*nxt)
                        if w in RANKS:
                            rank_of(*nxt, RANKS[w])
                        if w == SHARES:
                            shares(*nxt)

                for quarter in range(4):
                    inverse_denominators(0, 0, quarter)
                contexts_over_denominators(0, 0)
                low_weights(dve, nc.vector, 1)
                gate_attention(0, 0, 0)
                residual(0, 0)
                statistics(0, 0)
                normalise(0, 0)
                low_weights(dve, nc.vector, 3)
                modulate(0, 0, 0)
                low_h2(0, 0)
                low_weights(dve, nc.vector, 5)
                probabilities(0, 0)
                rank_of(0, 0, range(E))
                shares(0, 0)
                low_weights(dve, nc.vector, 7)
                step(0, 0, first=True)
                with dve.Fori(0, last) as i:
                    step(1, i)
                    step(0, i + 1)
                step(1, last, more=False)
                mixed(1, last, E - 1)

            @block.tensor
            def _(pe):
                pe.wait_ge(w_in, 32)

                def project(p, i):
                    pe.wait_ge(ctx_norm[p], FIRST + i + 1)
                    pe.wait_ge(r_exp[1 - p], FIRST + i + p)
                    for t in range(TT):
                        o = bank(6 + t // 2)[:, (t % 2) * D:(t % 2 + 1) * D]
                        for k in range(KK):
                            mm = nc.tensor.matmul(o, num[p][:, k, t * P:(t + 1) * P], wo_s[:, k, :],
                                                  start=(k == 0), stop=(k == KK - 1))
                        mm.then_inc(o_mm[p], 1)

                def transposes(p, i):
                    pe.wait_ge(res_done[p], FIRST + TT * (i + 1))
                    for k in range(KK):
                        for t in range(TT):
                            mm = nc.tensor.transpose(bank(6 + k)[:, t * P:(t + 1) * P],
                                                     xn[:, t, k * P:(k + 1) * P], ident[:, :])
                        mm.then_inc(t_mm[p], 1)

                def route(p, i):
                    pe.wait_ge(h_done[p], FIRST + KK * (i + 1))
                    for t in range(TT):
                        for k in range(KK):
                            mm = nc.tensor.matmul(bank(6)[:, t * E:(t + 1) * E], h2t[:, k, t * P:(t + 1) * P],
                                                  rw_s[:, k, :], start=(k == 0), stop=(k == KK - 1))
                    mm.then_inc(r_mm[p], 1)

                def up(p, i, w, first=False):
                    if w == 0:
                        pe.wait_ge(h_lo[p], FIRST + i + 1)
                    if w < 2 and not first:
                        pe.wait_ge(relu_done[1 - p], FIRST + NW * (i + p) + w - 1)
                    elif w >= 2:
                        pe.wait_ge(relu_done[p], FIRST + NW * i + w - 1)
                    cols = slice(w * P, (w + 1) * P)
                    for k in range(KK):
                        nc.tensor.matmul(bank(w % 2), w1_hi[:, k, cols], h2_hi[p][:, k, :],
                                         start=(k == 0), stop=False)
                        nc.tensor.matmul(bank(w % 2), w1_hi[:, k, cols], h2_lo[p][:, k, :], start=False, stop=False)
                        mm = nc.tensor.matmul(bank(w % 2), w1_lo[:, k, cols], h2_hi[p][:, k, :],
                                              start=False, stop=(k == KK - 1))
                    mm.then_inc(u_mm[p], 1)

                def down(p, i, w, first):
                    e = EXPERT[w]
                    low_parts_done(pe, p, i, w)
                    if w == FIRST_W[e]:
                        if e >= 2:
                            pe.wait_ge(mix_done[p], FIRST + TT * (E * i + e - 1))
                        elif not first:
                            pe.wait_ge(mix_done[1 - p], FIRST + TT * (E * (i + p) + e - 1))
                    for t in range(TT):
                        y = bank(2 + 2 * (e % 2) + t // 2)[:, (t % 2) * D:(t % 2 + 1) * D]
                        hi, lo = (h[w % HB][:, t * P:(t + 1) * P] for h in (hid_hi, hid_lo))
                        nc.tensor.matmul(y, hi, w2_hi[:, w, :], start=(w == FIRST_W[e] and t % 2 == 0),
                                         stop=False, skip_group_check=True)
                        nc.tensor.matmul(y, hi, w2_lo[:, w, :], start=False, stop=False, skip_group_check=True)
                        mm = nc.tensor.matmul(y, lo, w2_hi[:, w, :], start=False,
                                              stop=(w == FIRST_W[e] + FT[e] - 1), skip_group_check=True)
                    mm.then_inc(d_mm[p], 1)

                def step(p, i, first=False, more=True):
                    nxt = following(p, i)
                    for w in range(NW):
                        if w + 2 < NW:
                            up(p, i, w + 2)
                        elif more:
                            up(*nxt, w + 2 - NW)
                        if w >= 1:
                            down(p, i, w - 1, first)
                        elif not first:
                            down(*preceding(p, i), NW - 1, False)
                        if more and w == PROJECT:
                            project(*nxt)
                        if more and w == TRANSPOSE:
                            transposes(*nxt)
                        if more and w == ROUTE:
                            route(*nxt)

                project(0, 0)
                transposes(0, 0)
                route(0, 0)
                for k in range(2):
                    pe.wait_ge(w_lo[k], len(pieces) // 2)
                up(0, 0, 0, first=True)
                up(0, 0, 1, first=True)
                step(0, 0, first=True)
                with pe.Fori(0, last) as i:
                    step(1, i)
                    step(0, i + 1)
                step(1, last, more=False)
                down(1, last, NW - 1, False)


def kernel(L0_attn_x, L0_attn_W_qkv, L0_attn_W_o, L0_ffn_router_w, L0_ffn_w1, L0_ffn_w2, L0_c, L0_wmod):
    import numpy as np
    import concourse.bacc as bacc
    from concourse.bass_utils import run_bass_kernel_spmd

    laid = {
        "x": np.asarray(L0_attn_x).reshape(T, D),
        "wqkv_t": np.asarray(L0_attn_W_qkv).reshape(3 * D, D).T,
        "wo_t": np.asarray(L0_attn_W_o).T,
        "rw_t": np.asarray(L0_ffn_router_w).T,
        "w1": np.asarray(L0_ffn_w1),
        "w2": np.asarray(L0_ffn_w2),
        "c_t": np.asarray(L0_c).T,
        "wmod": np.asarray(L0_wmod),
    }
    nc = bacc.Bacc("TRN2", target_bir_lowering=False, num_devices=1)
    nc.disable_value_cache = True
    arrays, args = {}, []
    for name, a in laid.items():
        arrays[f"in_{name}"] = np.ascontiguousarray(a)
        args.append(nc.dram_tensor(f"in_{name}", a.shape, F32, kind="ExternalInput").ap())
    args.append(nc.dram_tensor("out_0", (T, D), F32, kind="ExternalOutput").ap())
    adaln_layer(nc, *args)
    r = run_bass_kernel_spmd(nc, [arrays], core_ids=[0])
    return r.results[0]["out_0"].reshape(B, S, D)
```
